# Optimizing a Trainium2 kernel written in Bass

```python
import numpy as np
import jax
import jax.numpy as jnp

def _softmax(x, axis=-1):
    return jax.nn.softmax(x, axis=axis)

def _gelu(x):
    return jax.nn.gelu(x, approximate=True)

def _silu(x):
    return jax.nn.silu(x)

def _sigmoid(x):
    return jax.nn.sigmoid(x)

def _layernorm(x, axis=-1, eps=1e-05):
    m = jnp.mean(x, axis=axis, keepdims=True)
    v = jnp.var(x, axis=axis, keepdims=True)
    return (x - m) / jnp.sqrt(v + eps)

def _scatter_add(tgt, idx, src, axis=0):
    return tgt.at[idx].add(src)

def _segment_sum(src, seg, n):
    return jax.ops.segment_sum(src, seg, n)
kernel_name = 'mk_decoder_preln_d1_seqx_r4_e311e0'

def setup_inputs(seed: int=0):
    np.random.seed(seed)
    _w = jnp.asarray

    def _rec_inputs():
        import jax
        import jax.numpy as jnp
        _rk = jax.random.key(seed)
        x = 2.818e-05 + 1 * jax.random.normal(jax.random.fold_in(_rk, 1), (4, 512, 512), jnp.float32)
        _lenS = 512 - jax.random.randint(jax.random.fold_in(_rk, 7), (4,), 0, max(1, 512 // 4) + 1, jnp.int32)
        _lenS2 = 512 - jax.random.randint(jax.random.fold_in(_rk, 8), (4,), 0, max(1, 512 // 4) + 1, jnp.int32)
        _ctx_1024P = jax.random.normal(jax.random.fold_in(_rk, 11), (4, 16, 256), jnp.float32)
        _ctx_1024c = jax.random.dirichlet(jax.random.fold_in(_rk, 511), 0.3 * jnp.ones((16,), jnp.float32), (4, 512))
        _ctx_1024t = jnp.einsum('bsk,bkd->bsd', _ctx_1024c, _ctx_1024P)
        _ctx_1024t = _ctx_1024t * jax.lax.rsqrt(jnp.mean(jnp.square(_ctx_1024t)) + 1e-12) * 0.953939
        ctx_1024 = 7.22013e-05 + 1.00017 * (_ctx_1024t + 0.3 * jax.random.normal(jax.random.fold_in(_rk, 611), (4, 512, 256), jnp.float32))
        return (x, ctx_1024)
    x, ctx_1024 = _rec_inputs()

    def _L0_attn_setup():
        import jax, jax.numpy as jnp
        import numpy as np
        B, T, D_MODEL = (4, 1024, 512)
        D_LATENT = 128
        D_COMP = 64
        THETA = 10000.0
        LN_EPS = 1e-05

        def _rope_tables(seq_len: int, dim: int):
            inv_freq = 1.0 / THETA ** (jnp.arange(0, dim, 2, dtype=jnp.float32) / dim)
            freqs = jnp.arange(seq_len, dtype=jnp.float32)[:, None] * inv_freq[None, :]
            cos = jnp.concatenate([jnp.cos(freqs), jnp.cos(freqs)], axis=-1)
            sin = jnp.concatenate([jnp.sin(freqs), jnp.sin(freqs)], axis=-1)
            return (cos, sin)

        def _rotate_half(x):
            x1, x2 = jnp.split(x, 2, axis=-1)
            return jnp.concatenate([-x2, x1], axis=-1)
        key = jax.random.key(seed)
        ks = jax.random.split(key, 8)
        s = 0.02
        return {'x': jax.random.normal(ks[0], (B, T, D_MODEL), dtype=jnp.float32), 'W_to_kv': jax.random.normal(ks[1], (D_LATENT, D_MODEL), dtype=jnp.float32) * s, 'W_compress': jax.random.normal(ks[2], (D_COMP, D_LATENT), dtype=jnp.float32) * s, 'ln_gamma': jnp.ones((D_COMP,), dtype=jnp.float32), 'ln_beta': jnp.zeros((D_COMP,), dtype=jnp.float32), 'W_q_comp': jax.random.normal(ks[3], (D_COMP, D_COMP), dtype=jnp.float32) * s, 'W_kv_comp': jax.random.normal(ks[4], (2 * D_COMP, D_COMP), dtype=jnp.float32) * s, 'W_comp2lat': jax.random.normal(ks[5], (D_LATENT, D_COMP), dtype=jnp.float32) * s, 'W_out_res': jnp.zeros((D_MODEL, D_LATENT), dtype=jnp.float32), 'b_out_res': jnp.zeros((D_MODEL,), dtype=jnp.float32)}
    _L0_attn_all = _L0_attn_setup()
    _L0_attn_in = {k: v for k, v in _L0_attn_all.items() if k in ('W_to_kv', 'W_compress', 'ln_gamma', 'ln_beta', 'W_q_comp', 'W_kv_comp', 'W_comp2lat', 'W_out_res', 'b_out_res')}
    del _L0_attn_all

    def _L0_xattn_setup():
        import jax, jax.numpy as jnp
        import numpy as np
        B_, L_, D_MODEL = (4, 512, 256)
        D_STATE, D_CONV, EXPAND = (16, 4, 2)
        D_INNER = EXPAND * D_MODEL
        DT_RANK = (D_MODEL + 15) // 16

        def silu(x):
            return x * jax.nn.sigmoid(x)
        key = jax.random.key(seed)
        ks = jax.random.split(key, 10)
        f32 = jnp.float32
        hidden_states = jax.random.normal(ks[0], (B_, L_, D_MODEL), dtype=f32)
        z = jax.random.normal(ks[1], (B_, D_INNER, L_), dtype=f32)
        in_proj_w = jax.random.normal(ks[2], (D_INNER, D_MODEL), dtype=f32) * 0.02
        conv_w = jax.random.normal(ks[3], (D_INNER, 1, D_CONV), dtype=f32) * 0.1
        conv_b = jax.random.normal(ks[4], (D_INNER,), dtype=f32) * 0.02
        x_proj_w = jax.random.normal(ks[5], (DT_RANK + 2 * D_STATE, D_INNER), dtype=f32) * 0.02
        dt_proj_w = jax.random.uniform(ks[6], (D_INNER, DT_RANK), dtype=f32, minval=-DT_RANK ** (-0.5), maxval=DT_RANK ** (-0.5))
        dt = jnp.exp(jax.random.uniform(ks[7], (D_INNER,), dtype=f32, minval=np.log(0.001), maxval=np.log(0.1)))
        dt_proj_b = jnp.log(jnp.expm1(dt))
        A_log = jnp.log(jnp.broadcast_to(jnp.arange(1, D_STATE + 1, dtype=f32), (D_INNER, D_STATE)))
        D = jnp.ones((D_INNER,), f32)
        return {'hidden_states': hidden_states, 'z': z, 'in_proj_w': in_proj_w, 'conv_w': conv_w, 'conv_b': conv_b, 'x_proj_w': x_proj_w, 'dt_proj_w': dt_proj_w, 'dt_proj_b': dt_proj_b, 'A_log': A_log, 'D': D}
    _L0_xattn_all = _L0_xattn_setup()
    _L0_xattn_in = {k: v for k, v in _L0_xattn_all.items() if k in ('in_proj_w', 'conv_w', 'conv_b', 'x_proj_w', 'dt_proj_w', 'dt_proj_b', 'A_log', 'D')}
    del _L0_xattn_all

    def _L0_ffn_setup():
        import jax, jax.numpy as jnp
        import numpy as np
        E = 32
        K = 4
        G = 4
        TG = 2
        H = 512
        F = 256
        FS = 512
        SCALE = 2.0
        B, S = (2, 256)
        N = B * S
        CAP = 2 * (N * K // E)

        def _gate(x, gate_w, gate_bias):
            logits = x @ gate_w.T
            scores = jax.nn.sigmoid(logits)
            sc = scores + gate_bias
            n = x.shape[0]
            grp = sc.reshape(n, G, E // G)
            group_scores = jax.lax.top_k(grp, 2)[0].sum(-1)
            _, gidx = jax.lax.top_k(group_scores, TG)
            gmask = jnp.zeros((n, G), sc.dtype).at[jnp.arange(n)[:, None], gidx].set(1.0)
            smask = jnp.repeat(gmask, E // G, axis=1)
            tmp = jnp.where(smask > 0, sc, 0.0)
            _, topk_idx = jax.lax.top_k(tmp, K)
            topk_w = jnp.take_along_axis(scores, topk_idx, axis=1)
            topk_w = topk_w / (topk_w.sum(-1, keepdims=True) + 1e-20)
            return (topk_idx, topk_w * SCALE)

        def _moe(x, topk_idx, topk_w, w1, w2, w3):
            n = x.shape[0]
            flat_e = topk_idx.reshape(-1)
            oh = jax.nn.one_hot(flat_e, E, dtype=jnp.int32)
            pos = (jnp.cumsum(oh, axis=0) * oh).sum(-1) - 1
            keep = pos < CAP
            slot = jnp.where(keep, pos, CAP)
            x_rep = jnp.repeat(x, K, axis=0)
            buf = jnp.zeros((E, CAP, H), x.dtype).at[flat_e, slot].set(x_rep, mode='drop')
            h = jax.nn.silu(jnp.einsum('ech,ehf->ecf', buf, w1)) * jnp.einsum('ech,ehf->ecf', buf, w3)
            ob = jnp.einsum('ecf,efh->ech', h, w2)
            y = ob[flat_e, jnp.minimum(slot, CAP - 1)]
            y = jnp.where(keep[:, None], y, 0.0)
            return (y.reshape(n, K, H) * topk_w[:, :, None]).sum(1)
        key = jax.random.key(seed)
        ks = jax.random.split(key, 9)
        w = 0.02
        return {'hidden_states': jax.random.normal(ks[0], (B, S, H), jnp.float32), 'gate_w': jax.random.normal(ks[1], (E, H), jnp.float32) * w, 'gate_bias': jax.random.normal(ks[2], (E,), jnp.float32) * w, 'w1': jax.random.normal(ks[3], (E, H, F), jnp.float32) * w, 'w2': jax.random.normal(ks[4], (E, F, H), jnp.float32) * w, 'w3': jax.random.normal(ks[5], (E, H, F), jnp.float32) * w, 'shared_gate': jax.random.normal(ks[6], (H, FS), jnp.float32) * w, 'shared_up': jax.random.normal(ks[7], (H, FS), jnp.float32) * w, 'shared_down': jax.random.normal(ks[8], (FS, H), jnp.float32) * w}
    _L0_ffn_all = _L0_ffn_setup()
    _L0_ffn_in = {k: v for k, v in _L0_ffn_all.items() if k in ('gate_w', 'gate_bias', 'w1', 'w2', 'w3', 'shared_gate', 'shared_up', 'shared_down')}
    del _L0_ffn_all
    return {'x': x, 'ctx_1024': ctx_1024, 'L0_attn_W_to_kv': _L0_attn_in['W_to_kv'], 'L0_attn_W_compress': _L0_attn_in['W_compress'], 'L0_attn_ln_gamma': _L0_attn_in['ln_gamma'], 'L0_attn_ln_beta': _L0_attn_in['ln_beta'], 'L0_attn_W_q_comp': _L0_attn_in['W_q_comp'], 'L0_attn_W_kv_comp': _L0_attn_in['W_kv_comp'], 'L0_attn_W_comp2lat': _L0_attn_in['W_comp2lat'], 'L0_attn_W_out_res': _L0_attn_in['W_out_res'], 'L0_attn_b_out_res': _L0_attn_in['b_out_res'], 'L0_xattn_in_proj_w': _L0_xattn_in['in_proj_w'], 'L0_xattn_conv_w': _L0_xattn_in['conv_w'], 'L0_xattn_conv_b': _L0_xattn_in['conv_b'], 'L0_xattn_x_proj_w': _L0_xattn_in['x_proj_w'], 'L0_xattn_dt_proj_w': _L0_xattn_in['dt_proj_w'], 'L0_xattn_dt_proj_b': _L0_xattn_in['dt_proj_b'], 'L0_xattn_A_log': _L0_xattn_in['A_log'], 'L0_xattn_D': _L0_xattn_in['D'], 'L0_ffn_gate_w': _L0_ffn_in['gate_w'], 'L0_ffn_gate_bias': _L0_ffn_in['gate_bias'], 'L0_ffn_w1': _L0_ffn_in['w1'], 'L0_ffn_w2': _L0_ffn_in['w2'], 'L0_ffn_w3': _L0_ffn_in['w3'], 'L0_ffn_shared_gate': _L0_ffn_in['shared_gate'], 'L0_ffn_shared_up': _L0_ffn_in['shared_up'], 'L0_ffn_shared_down': _L0_ffn_in['shared_down']}

def reference(x, ctx_1024, L0_attn_W_to_kv, L0_attn_W_compress, L0_attn_ln_gamma, L0_attn_ln_beta, L0_attn_W_q_comp, L0_attn_W_kv_comp, L0_attn_W_comp2lat, L0_attn_W_out_res, L0_attn_b_out_res, L0_xattn_in_proj_w, L0_xattn_conv_w, L0_xattn_conv_b, L0_xattn_x_proj_w, L0_xattn_dt_proj_w, L0_xattn_dt_proj_b, L0_xattn_A_log, L0_xattn_D, L0_ffn_gate_w, L0_ffn_gate_bias, L0_ffn_w1, L0_ffn_w2, L0_ffn_w3, L0_ffn_shared_gate, L0_ffn_shared_up, L0_ffn_shared_down):
    import jax
    import jax.numpy as jnp

    def _L0_attn_ref(x, W_to_kv, W_compress, ln_gamma, ln_beta, W_q_comp, W_kv_comp, W_comp2lat, W_out_res, b_out_res):
        import jax, jax.numpy as jnp
        import numpy as np
        B, T, D_MODEL = (4, 1024, 512)
        D_LATENT = 128
        D_COMP = 64
        THETA = 10000.0
        LN_EPS = 1e-05

        def _rope_tables(seq_len: int, dim: int):
            inv_freq = 1.0 / THETA ** (jnp.arange(0, dim, 2, dtype=jnp.float32) / dim)
            freqs = jnp.arange(seq_len, dtype=jnp.float32)[:, None] * inv_freq[None, :]
            cos = jnp.concatenate([jnp.cos(freqs), jnp.cos(freqs)], axis=-1)
            sin = jnp.concatenate([jnp.sin(freqs), jnp.sin(freqs)], axis=-1)
            return (cos, sin)

        def _rotate_half(x):
            x1, x2 = jnp.split(x, 2, axis=-1)
            return jnp.concatenate([-x2, x1], axis=-1)
        Bx, Tx, _ = x.shape
        dc = W_compress.shape[0]
        kv_latent = x @ W_to_kv.T
        c = kv_latent @ W_compress.T
        mu = jnp.mean(c, axis=-1, keepdims=True)
        var = jnp.mean((c - mu) ** 2, axis=-1, keepdims=True)
        ch = (c - mu) * jax.lax.rsqrt(var + LN_EPS) * ln_gamma + ln_beta
        q = ch @ W_q_comp.T
        kv = ch @ W_kv_comp.T
        k, v = jnp.split(kv, 2, axis=-1)
        cos, sin = _rope_tables(Tx, dc)
        q = q * cos + _rotate_half(q) * sin
        k = k * cos + _rotate_half(k) * sin
        scale = 1.0 / jnp.sqrt(jnp.float32(dc))
        scores = jnp.einsum('btd,bsd->bts', q, k) * scale
        causal = jnp.tril(jnp.ones((Tx, Tx), dtype=bool))
        scores = jnp.where(causal[None], scores, jnp.float32(-1e+30))
        attn = jax.nn.softmax(scores, axis=-1)
        o = jnp.einsum('bts,bsd->btd', attn, v)
        z = o @ W_comp2lat.T
        out = z @ W_to_kv + z @ W_out_res.T + b_out_res
        return out

    def _L0_xattn_ref(hidden_states, z, in_proj_w, conv_w, conv_b, x_proj_w, dt_proj_w, dt_proj_b, A_log, D):
        import jax, jax.numpy as jnp
        import numpy as np
        B_, L_, D_MODEL = (4, 512, 256)
        D_STATE, D_CONV, EXPAND = (16, 4, 2)
        D_INNER = EXPAND * D_MODEL
        DT_RANK = (D_MODEL + 15) // 16

        def silu(x):
            return x * jax.nn.sigmoid(x)
        Bsz, L, _ = hidden_states.shape
        d_inner, _, d_conv = conv_w.shape
        dt_rank = dt_proj_w.shape[1]
        d_state = A_log.shape[1]
        x = jnp.einsum('bld,ed->bel', hidden_states, in_proj_w)
        xc = jax.lax.conv_general_dilated(x, conv_w, window_strides=(1,), padding=[(d_conv - 1, 0)], feature_group_count=d_inner, dimension_numbers=('NCH', 'OIH', 'NCH'))
        x = silu(xc + conv_b[None, :, None])
        x_dbl = jnp.einsum('bdl,ed->bel', x, x_proj_w)
        dt_low, Bm, Cm = jnp.split(x_dbl, [dt_rank, dt_rank + d_state], axis=1)
        dt = jnp.einsum('brl,dr->bdl', dt_low, dt_proj_w)
        dt = jax.nn.softplus(dt + dt_proj_b[None, :, None])
        A = -jnp.exp(A_log)
        dt_t = jnp.moveaxis(dt, -1, 0)
        B_t = jnp.moveaxis(Bm, -1, 0)
        C_t = jnp.moveaxis(Cm, -1, 0)
        u_t = jnp.moveaxis(x, -1, 0)

        def step(state, inp):
            d, b, c, u = inp
            dA = jnp.exp(d[..., None] * A)
            state = state * dA + (d * u)[..., None] * b[:, None, :]
            y = jnp.einsum('bdn,bn->bd', state, c)
            return (state, y)
        state0 = jnp.zeros((Bsz, d_inner, d_state), x.dtype)
        _, ys = jax.lax.scan(step, state0, (dt_t, B_t, C_t, u_t))
        y = jnp.moveaxis(ys, 0, 2)
        y = y + D[None, :, None] * x
        y = y * silu(z)
        return jnp.swapaxes(y, 1, 2)

    def _L0_ffn_ref(hidden_states, gate_w, gate_bias, w1, w2, w3, shared_gate, shared_up, shared_down):
        import jax, jax.numpy as jnp
        import numpy as np
        E = 32
        K = 4
        G = 4
        TG = 2
        H = 512
        F = 256
        FS = 512
        SCALE = 2.0
        B, S = (2, 256)
        N = B * S
        CAP = 2 * (N * K // E)

        def _gate(x, gate_w, gate_bias):
            logits = x @ gate_w.T
            scores = jax.nn.sigmoid(logits)
            sc = scores + gate_bias
            n = x.shape[0]
            grp = sc.reshape(n, G, E // G)
            group_scores = jax.lax.top_k(grp, 2)[0].sum(-1)
            _, gidx = jax.lax.top_k(group_scores, TG)
            gmask = jnp.zeros((n, G), sc.dtype).at[jnp.arange(n)[:, None], gidx].set(1.0)
            smask = jnp.repeat(gmask, E // G, axis=1)
            tmp = jnp.where(smask > 0, sc, 0.0)
            _, topk_idx = jax.lax.top_k(tmp, K)
            topk_w = jnp.take_along_axis(scores, topk_idx, axis=1)
            topk_w = topk_w / (topk_w.sum(-1, keepdims=True) + 1e-20)
            return (topk_idx, topk_w * SCALE)

        def _moe(x, topk_idx, topk_w, w1, w2, w3):
            n = x.shape[0]
            flat_e = topk_idx.reshape(-1)
            oh = jax.nn.one_hot(flat_e, E, dtype=jnp.int32)
            pos = (jnp.cumsum(oh, axis=0) * oh).sum(-1) - 1
            keep = pos < CAP
            slot = jnp.where(keep, pos, CAP)
            x_rep = jnp.repeat(x, K, axis=0)
            buf = jnp.zeros((E, CAP, H), x.dtype).at[flat_e, slot].set(x_rep, mode='drop')
            h = jax.nn.silu(jnp.einsum('ech,ehf->ecf', buf, w1)) * jnp.einsum('ech,ehf->ecf', buf, w3)
            ob = jnp.einsum('ecf,efh->ech', h, w2)
            y = ob[flat_e, jnp.minimum(slot, CAP - 1)]
            y = jnp.where(keep[:, None], y, 0.0)
            return (y.reshape(n, K, H) * topk_w[:, :, None]).sum(1)
        b, s, h = hidden_states.shape
        x = hidden_states.reshape(-1, h)
        topk_idx, topk_w = _gate(x, gate_w, gate_bias)
        out = _moe(x, topk_idx, topk_w, w1, w2, w3)
        shared = jax.nn.silu(x @ shared_gate) * (x @ shared_up) @ shared_down
        return (out + shared).reshape(b, s, h)
    x = x + _L0_attn_ref(_layernorm(x, axis=-1), L0_attn_W_to_kv, L0_attn_W_compress, L0_attn_ln_gamma, L0_attn_ln_beta, L0_attn_W_q_comp, L0_attn_W_kv_comp, L0_attn_W_comp2lat, L0_attn_W_out_res, L0_attn_b_out_res)
    x = x + _L0_xattn_ref(ctx_1024, _layernorm(x, axis=-1), L0_xattn_in_proj_w, L0_xattn_conv_w, L0_xattn_conv_b, L0_xattn_x_proj_w, L0_xattn_dt_proj_w, L0_xattn_dt_proj_b, L0_xattn_A_log, L0_xattn_D)
    x = x + _L0_ffn_ref(_layernorm(x, axis=-1), L0_ffn_gate_w, L0_ffn_gate_bias, L0_ffn_w1, L0_ffn_w2, L0_ffn_w3, L0_ffn_shared_gate, L0_ffn_shared_up, L0_ffn_shared_down)
    return x

_drawn_inputs = setup_inputs


def setup_inputs(seed=0):
    import zlib

    import numpy as np

    out = dict(_drawn_inputs(seed))
    spreads = {'L0_attn_ln_gamma': (1.0, 0.6),
     'L0_attn_ln_beta': (0.0, 0.8),
     'L0_attn_W_out_res': (0.0, 0.8),
     'L0_attn_b_out_res': (0.0, 0.8),
     'L0_xattn_D': (1.0, 0.6)}
    factors = {'ctx_1024': 2.817,
     'L0_attn_W_to_kv': 8.0,
     'L0_attn_W_compress': 8.0,
     'L0_attn_W_q_comp': 8.0,
     'L0_attn_W_kv_comp': 8.0,
     'L0_attn_W_comp2lat': 8.0,
     'L0_xattn_in_proj_w': 2.826,
     'L0_xattn_conv_w': 2.881,
     'L0_xattn_conv_b': 8.0,
     'L0_xattn_x_proj_w': 8.0,
     'L0_xattn_dt_proj_w': 8.0,
     'L0_xattn_dt_proj_b': 8.0,
     'L0_xattn_A_log': 8.0,
     'L0_ffn_gate_bias': 33.144,
     'L0_ffn_gate_w': 8.0,
     'L0_ffn_w1': 8.0,
     'L0_ffn_w2': 8.0,
     'L0_ffn_w3': 8.0,
     'L0_ffn_shared_gate': 8.0,
     'L0_ffn_shared_up': 8.0,
     'L0_ffn_shared_down': 8.0}
    for name, (base, spread) in spreads.items():
        noise = np.random.default_rng([zlib.crc32(name.encode()), seed]).standard_normal(out[name].shape)
        drawn = base * np.exp(spread * noise) if base else spread * noise
        out[name] = jnp.asarray(drawn.astype(out[name].dtype))
    for name, factor in factors.items():
        out[name] = (out[name] * factor).astype(out[name].dtype)
    return out
```

```python
from contextlib import ExitStack

import numpy as np

import concourse.bass as bass
from concourse import mybir

ALU = mybir.AluOpType
ACT = mybir.ActivationFunctionType
F32 = mybir.dt.float32
BF16 = mybir.dt.bfloat16
U32 = mybir.dt.uint32
AX_X = mybir.AxisListType.X

P = 128
B, T, D = 4, 512, 512
TT = T // P
KD = D // P
DC, DCTX, NS, RK = 64, 256, 16, 16
DI = 512
CH = DI // P
E, TOPK, G, CAP = 32, 4, 4, 128
FE, FS = 256, 512
KF = FS // P
EPS = 1e-5
NEG = -1e30
STEPS = CH * NS
NK = B * STEPS
ROW = D + 16
W_AT, E_AT, ID_AT = D, D + TOPK, D + 2 * TOPK
FAR = 1.0e6
AHEAD_ACT, AHEAD_POOL = 1, 2
FOLD_AT = (-1, 16)
N_DA, N_CB, N_DBU, N_H, N_HC, N_DT = 2, 2, 3, 2, 3, 7

N_ROUTE, N_SLOTS, N_SPLIT = 20, 6, 4
CHOSEN, SCORED = 15, 17

COUNT = {
    "in_proj": 4, "x_proj": 1, "dt_proj": 4, "b_bcast": NS, "ln0_T": 4, "c_proj": 1, "c_T": 1,
    "qk": 1, "qk_rolled": 1, "v": 1, "score": 4, "p_T": 4, "pv": 4, "attn_out": 4, "y_T": 4,
    "ln2_T": 4, "logits": 1, "earlier": 1, "ffn_gate": 4, "ffn_up": 4, "ffn_down": 4,
    "c_bcast": STEPS, "state_sum": STEPS,
    "u_copy": 4, "conv_first": 4, "conv_tanh": 4, "x_copy": 1, "dt_exp": 4, "ln": 1, "b_copy": NS,
    "ln0_norm": 4, "ln0_T_copy": 4, "c_copy": 1, "c_affine": 1, "v_copy": 1, "p_exp": 4, "p_T_copy": 4, "pv_copy": 4,
    "g_norm": 4, "g_tanh": 4, "ln2_norm": 4, "ln2_T_copy": 4, "logits_tanh": 1, "ffn_tanh": 4, "decay": STEPS,
    "conv": 12, "u_gate": 4, "split": N_SPLIT, "e_round": 4, "dt": 4, "dtu": 4, "ln0_stats": 4,
    "ln0_aggr": 4, "c_stats": 1, "c_aggr": 1, "c_norm": 1, "rope_cos": 1, "rope_sin": 1, "rope_add": 2,
    "score_mask": 4, "score_max": 4, "score_neg": 4, "p_recip": 4, "x1": 4, "x1_stats": 4, "x1_aggr": 4,
    "g_mul": 4, "y_sum": 4, "y_gate": 4, "y_add": 4, "ln2_stats": 4, "ln2_aggr": 4,
    "route": N_ROUTE, "slots": N_SLOTS, "ffn_silu": 4, "ffn_h": 4, "ffn_add": 4,
    "scan": STEPS, "times_c": STEPS,
    "scan_in": STEPS, "e_rest": 4, "log1p": 4, "x_bias": 4, "ln0_rstd": 4, "c_rstd": 1, "x1_rstd": 1, "ln2_rstd": 1,
}

PLAN = {"pe": [], "act": [], "dve": [], "pool": []}
BANK = {}

ROOM = {"pe": 2.6, "act": 2.6, "dve": 1.3, "pool": 1.5}
LAG = {"dve": {"dve": 0.5, "act": 1, "pool": 1, "pe": 1}, "act": {"dve": 1, "act": 0, "pool": 1, "pe": 1},
       "pool": {"dve": 0.5, "act": 0.5, "pool": 0, "pe": 1}, "pe": {"dve": 1, "act": 1, "pool": 1, "pe": 0}}
GENERAL = (5, 6, 7)
FIRST_GATE, ATTENTION = 4, -64
SHARED_DOWN, SHARED_IN = 64, 64
SPARE = {("c_aggr", 0): 0.5, ("x1", 0): 0.5, ("x1", 1): 0.5, ("x1", 2): 0.5, ("x1", 3): 0.5, ("c_rstd", 0): 1,
         ("x1_aggr", 2): 2, ("rope_add", 1): 2, ("split", 0): 0.5, ("split", 1): 0.5, ("split", 2): 0.5,
         ("split", 3): 0.5, ("dt_exp", 2): 1, ("dtu", 1): 1.5, ("ffn_add", 0): 2, ("ffn_add", 1): 2,
         ("ffn_add", 2): 2, ("ffn_add", 3): 2, ("ffn_h", 0): 1, ("ffn_h", 1): 1, ("ffn_h", 2): 1, ("ffn_h",
         3): 1, ("y_gate", 0): 1, ("y_gate", 1): 1, ("y_gate", 2): 1, ("y_gate", 3): 1}


def _plan():
    load = {}
    at = {}
    held = {}
    engine_of = {}

    def slot(engine, step):
        return engine, step % STEPS

    def first_step(engine, step, after):
        for key in after:
            shift = 0
            if len(key) == 3:
                key, shift = key[:2], key[2]
            step = max(step, at[key] + shift + LAG[engine_of[key]][engine])
        return step if engine == "dve" else int(-(-step // 1))

    def steps_from(start, items):
        where, step = [], start
        for j, (engine, task, i, cost, after) in enumerate(items):
            lag = LAG[items[j - 1][0]][engine] if j else 0
            step = first_step(engine, ((where[-1] + lag) if j else step), after)
            step += SPARE.get((task, i), 0)
            while True:
                used = load.get(slot(engine, step), 0.0)
                used += sum(it[3] for it, w in zip(items, where) if it[0] == engine and (w - step) % STEPS == 0)
                if used == 0.0 or used + cost <= ROOM[engine]:
                    break
                step += 0.5 if engine == "dve" else 1
            where.append(step)
        return where

    def chain(start, items, bank=None):
        where = steps_from(start, items)
        while bank:
            late = steps_from(where[0] + 1, items)
            while late[-1] == where[-1]:
                where, late = late, steps_from(late[0] + 1, items)
            until = int(where[bank[1]]) + (items[bank[1]][0] == "dve")
            span = [st % STEPS for st in range(int(where[bank[0]]), until)]
            free = [g for g in GENERAL if not any((g, st) in held for st in span)]
            if free:
                idle = lambda g: next((n for n in range(1, STEPS) if (g, (span[0] - n) % STEPS) in held), STEPS)
                chosen = max(free, key=idle)
                for st in span:
                    held[(chosen, st)] = True
                BANK[items[bank[0]][1:3]] = chosen
                break
            if where[0] > 4 * STEPS:
                raise ValueError(f"no PSUM bank is free for {items[0]}")
            where = late
        for (engine, task, i, cost, after), step in zip(items, where):
            load[slot(engine, step)] = load.get(slot(engine, step), 0.0) + cost
            at[(task, i)] = step
            engine_of[(task, i)] = engine
            PLAN[engine].append((step % STEPS, int(-(step // STEPS)), task, i))

    for c in range(CH):
        done_at = NS * (c + 1)
        chain(done_at + 1.5, [("dve", "y_sum", c, 0.6, [])])
        chain(done_at + (FIRST_GATE if c == 0 else 1), [("dve", "y_gate", c, 0.6, [("y_sum", c)]),
                            ("pe", "y_T", c, 0.43, []), ("dve", "y_add", c, 0.6, [])], (1, 2))
    for n in range(NS):
        chain(n - NS - 1, [("pe", "b_bcast", n, 0.22, []), ("act", "b_copy", n, 0.5, [])], (0, 1))
    for c in range(CH):
        again = [("conv", 3 * c - 1)] if c else []
        chain(4 - STEPS + 2 * c, [("pe", "in_proj", c, 1.7, []), ("act", "u_copy", c, 0.5, again)], (0, 1))
        chain(-STEPS, [("act", "conv_first", c, 0.6, [("u_copy", c)]),
                       ("dve", "conv", 3 * c, 0.6, []), ("dve", "conv", 3 * c + 1, 0.6, []), ("dve", "conv", 3 * c + 2, 0.6, []),
                       ("act", "conv_tanh", c, 0.5, [("u_gate", c - 1)] if c else []), ("dve", "u_gate", c, 0.6, [])])
    chain(-STEPS, [("pe", "x_proj", 0, 1.7, [("u_gate", CH - 1)]), ("act", "x_copy", 0, 0.5, [])], (0, 1))
    chain(-STEPS, [("dve", "split", j, 0.6 if j else 0.3, [("x_copy", 0)]) for j in range(N_SPLIT)])
    for c in range(CH):
        chain(-STEPS, [("pe", "dt_proj", c, 0.85, [("x_copy", 0)]), ("act", "dt_exp", c, 1.6, [("split", N_SPLIT - 1)])], (0, 1))
        chain(-STEPS, [("dve", "e_round", c, 0.6, [("dt_exp", c)]), ("pool", "e_rest", c, 1.2, [])])
    chain(-STEPS, [("act", "ln", 0, 1.8, [("e_rest", c) for c in range(CH)])])
    for c in range(CH):
        chain(-STEPS, [("pool", "log1p", c, 1.2, [("ln", 0)]), ("dve", "dt", c, 0.6, [])])
        chain(NS * (c + 1) - STEPS - 1, [("dve", "dtu", c, 0.6, [("dt", c)])])
    last = [("y_add", CH - 1)]
    for t in range(TT):
        chain(STEPS, [("dve", "ln2_stats", t, 0.6, last), ("dve", "ln2_aggr", t, 0.1, [])])
    chain(STEPS, [("pool", "ln2_rstd", 0, 0.3, [("ln2_aggr", TT - 1)])])
    for t in range(TT):
        chain(STEPS, [("act", "ln2_norm", t, 0.6, [("ln2_rstd", 0)])])
        chain(STEPS, [("pe", "ln2_T", t, 0.43, [("ln2_norm", t)]), ("act", "ln2_T_copy", t, 0.5, [])], (0, 1))
    copied = [("ln2_T_copy", TT - 1)]
    chain(STEPS, [("pe", "logits", 0, 1.7, copied), ("act", "logits_tanh", 0, 0.3, [])], (0, 1))
    for f in range(KF):
        before = [("ffn_h", f - 1)] if f else []
        chain(SHARED_IN, [("pe", "ffn_gate_lo", f, 1.7, copied), ("pe", "ffn_gate", f, 1.7, []),
                      ("act", "ffn_tanh", f, 0.5, before), ("dve", "ffn_silu", f, 0.6, [])], (0, 3))
        chain(STEPS, [("pe", "ffn_up_lo", f, 1.7, [("ffn_gate", f)]), ("pe", "ffn_up", f, 1.7, []),
                      ("dve", "ffn_h", f, 0.6, [("ffn_silu", f)])], (0, 2))
    for t in range(TT):
        chain(SHARED_DOWN + 2 * t, [("pe", "ffn_down_lo", t, 1.7, [("ffn_h", KF - 1)]), ("pe", "ffn_down", t, 1.7, []),
                      ("dve", "ffn_add", t, 0.6, [])], (0, 2))
    for t in range(TT):
        chain(-44 + 0 * t, [("dve", "ln0_stats", t, 0.6, [("ln0_T", t - 2, 3)] if t >= 2 else []), ("dve", "ln0_aggr", t, 0.1, []), ("pool", "ln0_rstd", t, 0.3, []),
                      ("act", "ln0_norm", t, 0.6, [])])
        chain(-STEPS, [("pe", "ln0_T", t, 0.43, [("ln0_norm", t)]),
                       ("act", "ln0_T_copy", t, 0.5, [("ffn_up", KF - 1, -2 * STEPS)])], (0, 1))
    chain(ATTENTION, [("pe", "c_proj", 0, 1.7, [("ln0_T_copy", TT - 1), ("dt", CH - 1)]), ("act", "c_copy", 0, 0.4, [])], (0, 1))
    chain(-STEPS, [("dve", "c_stats", 0, 0.5, [("c_copy", 0)]), ("dve", "c_aggr", 0, 0.3, []), ("pool", "c_rstd", 0, 0.3, []), ("dve", "c_norm", 0, 0.6, [])])
    chain(-STEPS, [("pe", "c_T", 0, 0.43, [("c_norm", 0)]), ("act", "c_affine", 0, 0.6, [])], (0, 1))
    for task, reader in (("qk", "rope_cos"), ("qk_rolled", "rope_sin")):
        chain(-STEPS, [("pe", task, 0, 0.85, [("c_affine", 0)]), ("dve", reader, 0, 0.6, [])], (0, 1))
    chain(-STEPS, [("dve", "rope_add", j, 0.6, [("rope_cos", 0), ("rope_sin", 0)]) for j in range(2)])
    chain(-STEPS, [("pe", "v", 0, 0.5, [("c_affine", 0)]), ("act", "v_copy", 0, 0.5, [])], (0, 1))
    for t in range(TT):
        chain(-12 + 2 * t, [("pool", "x_bias", t, 1.2, [("ffn_add", TT - 1, 3 - 2 * STEPS)])])
    for t in range(TT):
        chain(-STEPS, [("pe", "score", t, 0.6, [("rope_add", 1)]), ("dve", "score_mask", t, 0.2, []),
                       ("dve", "score_max", t, 0.6, []), ("dve", "score_neg", t, 0.1, []),
                       ("act", "p_exp", t, 0.6, [("p_T", t - 2)] if t >= 2 else [("ffn_down", TT - 1, -2 * STEPS)])], (0, 4))
        chain(-STEPS, [("pe", "p_T", t, 0.43, [("p_exp", t)]),
                       ("act", "p_T_copy", t, 0.5, [("pv", t - 2)] if t >= 2 else [])], (0, 1))
        chain(-STEPS, [("dve", "p_recip", t, 0.1, [("p_exp", t)])])
        chain(-STEPS, [("pe", "pv", t, 0.6, [("p_T_copy", t), ("v_copy", 0)]), ("act", "pv_copy", t, 0.2, [])], (0, 1))
        chain(-STEPS, [("pe", "attn_out", t, 0.85, [("pv_copy", t)]), ("dve", "x1", t, 0.6, [("x_bias", t), ("p_recip", t)])], (0, 1))
        chain(-STEPS, [("dve", "x1_stats", t, 0.6, [("x1", t)]), ("dve", "x1_aggr", t, 0.1, [])])
    chain(-STEPS, [("pool", "x1_rstd", 0, 0.3, [("x1_aggr", TT - 1)])])
    for c in range(CH):
        chain(-STEPS, [("act", "g_norm", c, 0.6, [("x1_rstd", 0)])])
        at_least = NS * c + 6
        chain(at_least, [("act", "g_tanh", c, 0.5, [("g_norm", c)] + ([("y_gate", c - 1)] if c else [("y_gate", CH - 1, -STEPS)])),
                         ("dve", "g_mul", c, 0.6, [])])
    chain(STEPS, [("dve", "route", j, 0.3, [("logits_tanh", 0)]) for j in range(N_ROUTE)])
    chain(STEPS, [("pe", "earlier", 0, 0.5, [("route", CHOSEN)]), ("dve", "slots", 0, 0.5, [("route", SCORED)])], (0, 1))
    chain(STEPS, [("dve", "slots", j, 0.3, [("slots", 0), ("route", N_ROUTE - 1)]) for j in range(1, N_SLOTS)])
    for j in range(TT * TOPK):
        chain(STEPS, [("pool", "scatter", j, 1.1, [("slots", N_SLOTS - 1)])])
    for engine in PLAN:
        PLAN[engine].sort(key=lambda x: x[0])


_plan()

READER = {
    "in_proj": "u_copy", "x_proj": "x_copy", "dt_proj": "dt_exp", "b_bcast": "b_copy",
    "ln0_T": "ln0_T_copy", "c_proj": "c_copy", "c_T": "c_affine", "qk": "rope_cos",
    "qk_rolled": "rope_sin", "v": "v_copy", "score": "p_exp", "p_T": "p_T_copy", "pv": "pv_copy",
    "attn_out": "x1", "y_T": "y_add", "ln2_T": "ln2_T_copy", "logits": "logits_tanh",
    "earlier": "slots", "ffn_gate_lo": "ffn_silu", "ffn_up_lo": "ffn_h", "ffn_down_lo": "ffn_add",
}


def side_work(engine, phase, step):
    return [(task, phase + off, i) for s, off, task, i in PLAN[engine]
            if s == step and 0 <= phase + off < B]


def _last_users():
    held, out = {}, {}
    for phase in range(-1, B + 2):
        for step in range(STEPS):
            for task, b, i in side_work("pe", phase, step):
                if (task, i) in BANK:
                    bank = BANK[(task, i)]
                    out[(task, b, i)] = held.get(bank)
                    held[bank] = (task, b, i)
    return out


BEFORE = _last_users()


def decoder_layer(nc, x, ctx_t, lat_w, comp_w, qk_w, in_w, xp_w, dtp_w, chan, gate_w, token_b,
                  shared_w, expert_w, const_f, const_b, out, rows_dram):
    stack = ExitStack()
    with stack:
        def sem(name):
            return stack.enter_context(nc.semaphore(name))

        S = {task: sem(f"s_{task}") for task in COUNT}

        def done(task, b, i=0):
            return S[task], b * COUNT[task] + i + 1

        inner_in = sem("inner_in")
        weights_in = sem("weights_in")
        shared_in = [sem(f"shared_in{i}") for i in range(2)]
        down_in = [sem(f"down_in{i}") for i in range(2)]
        rows_zeroed = sem("rows_zeroed")
        ctx_in = sem("ctx_in")
        x_tile_in = [sem(f"x_tile_in{i}") for i in range(2)]
        x_batch_in = [sem(f"x_batch_in{i}") for i in range(2)]
        scattered = sem("scattered")
        stored = sem("stored")
        weff_psum = sem("weff_psum")
        folded = sem("folded")
        dve_own = sem("dve_own")
        act_own = sem("act_own")
        pool_own = sem("pool_own")
        setup = sem("setup")
        lat_summed = sem("lat_summed")

        with ExitStack() as first:
            def sb(name, shape, dt=F32):
                return first.enter_context(nc.sbuf_tensor(name, shape, dt))

            banks = [first.enter_context(nc.psum_tensor(f"bank{i}", [P, 512], F32)) for i in range(8)]
            decay_ps, cb_ps, y_ps = banks[0:2], banks[2:4], banks[4]

            cmp_w = sb("cmp_w", [P, 2 * DC + 2])
            wqk = sb("wqk", [DC, 2 * P + DC])
            inw = sb("inw", [P, DCTX // P, DI])
            xpw = sb("xpw", [P, CH, DC])
            dtw = sb("dtw", [RK, DI])
            chn_w = sb("chn_w", [P, CH, 7 + NS])
            gw = sb("gw", [P, KD, E])
            tokb = sb("tokb", [P, D + E])
            shw = sb("shw", [P, 2, 2, KD * P])
            sh_down = shw[:, :, :, :].rearrange("p s w n -> p (s w n)")
            cf = sb("cf", [P, P + P + 2 * T + 3 * E + TT * B])
            cb16 = sb("cb16", [P, 2 * P + E], BF16)
            ident = cf[:, 0:P]
            cmask = cf[:, P:2 * P]
            cos = cf[:, 2 * P:2 * P + T]
            sin = cf[:, 2 * P + T:2 * P + 2 * T]
            at = 2 * P + 2 * T
            iota_e = cf[:, at:at + E]
            iota_g = cf[:, at + E:at + 2 * E]
            tok_id = cf[:, at + 3 * E:at + 3 * E + TT * B]
            before = cb16[:, 0:P]
            ones = cb16[:, P:2 * P]
            pick = cb16[0:96, 2 * P:2 * P + E]
            bias_out = tokb[:, 0:D]
            bias_gate = tokb[:, D:D + E]
            conv_w = lambda c, j: chn_w[:, c, j:j + 1]
            conv_b = lambda c: chn_w[:, c, 4:5]
            dt_b = lambda c: chn_w[:, c, 5:6]
            skip_d = lambda c: chn_w[:, c, 6:7]
            a_log = chn_w[:, :, 7:7 + NS]
            a_neg = sb("a_neg", [P, CH, NS])
            weff = sb("weff", [P, KD, DC])
            wout = sb("wout", [DC, D])

            base = sb("base", [P, 2, TT, D])
            rowx = sb("rowx", [P, TT, ROW])
            xT = sb("xT", [P, KD, T])
            b_all = sb("b_all", [P, NS, T])
            scan_in = sb("scan_in", [P, N_DBU, T])
            state = sb("state", [P, N_H, T])
            state_c = sb("state_c", [P, N_HC, T])
            dt_ring = sb("dt_ring", [P, N_DT, T])
            dtu = sb("dtu", [P, CH, T])
            u2 = sb("u2", [P, 2, CH, T])
            gx = sb("gx", [P, CH, T])
            lat = gx[:, 0:2, :].rearrange("p a d -> p (a d)")
            gt = sb("gt", [P, T])
            ybuf = sb("ybuf", [P, T])
            dt_of = lambda b, c: dt_ring[:, (b * CH + c) % N_DT, :]
            upad = sb("upad", [P, T + 3])
            cth = sb("cth", [P, T])
            xd = sb("xd", [DC, T])
            bc_parts = sb("bc_parts", [96, 2, T], BF16)
            turn_a = sb("turn_a", [P, 4, T])
            turn_b = sb("turn_b", [P, 4, T])
            e4, c4 = turn_a, turn_b
            bc_rest, bc_mid = turn_a[:, 0, :], turn_a[:, 1, 0:T // 2].bitcast(BF16)
            r_cos, r_sin, qT, kT = turn_a[:, 0, :], turn_a[:, 1, :], turn_a[0:DC, 2, :], turn_a[0:DC, 3, :]
            chT, oT = turn_b[0:DC, 0, :], turn_b[0:DC, 1, :]
            v_sb = turn_b[:, 2, 0:TT * DC].rearrange("p (t c) -> p t c", c=DC)
            cn = turn_b[:, 2, TT * DC:2 * TT * DC].rearrange("p (t c) -> p t c", c=DC)
            turn_c = sb("turn_c", [P, 4, T])
            hT = turn_c
            probs, probsT = turn_c[:, 0:2, :], turn_c[:, 2:4, :]
            xr = sb("xr", [P, 2, T])
            ctxT = xr
            fth = sb("fth", [P, T])
            st6 = sb("st6", [P, 4, TT, 6])
            mv0 = sb("mv0", [P, TT, 2])
            mvc = sb("mvc", [P, TT, 2])
            mv1 = sb("mv1", [P, TT, 2])
            mv2 = sb("mv2", [P, TT, 2])
            rs0, rsc, rs1, rs2 = (sb(f"rs{i}", [P, TT]) for i in range(4))
            nb0, nb1, nb2 = (sb(f"nb{i}", [P, TT]) for i in range(3))
            mhalf = sb("mhalf", [P, TT])
            nmax = sb("nmax", [P, TT])
            psums = sb("psums", [P, TT])
            prec = sb("prec", [P, TT])
            score = sb("score", [P, TT, E])
            score_b = sb("score_b", [P, TT, E])
            kept = sb("kept", [P, TT, E])
            kept2 = sb("kept2", [P, TT, E])
            m8 = sb("m8", [P, TT * G, 8])
            gs8 = sb("gs8", [P, TT, 8])
            g8 = sb("g8", [P, TT, 8])
            gi = sb("gi", [P, TT, 8], U32)
            gif = sb("gif", [P, TT, 2])
            t8 = sb("t8", [P, TT, 8])
            ti = sb("ti", [P, TT, 8], U32)
            eif = sb("eif", [P, TT * TOPK])
            hot = sb("hot", [P, TT * TOPK, E])
            prod = sb("prod", [P, TT * TOPK, E])
            chosen = sb("chosen", [P, TT, E], BF16)
            seen = sb("seen", [P, E], BF16)
            wraw = sb("wraw", [P, TT * TOPK])
            wsum = sb("wsum", [P, TT])
            pos = sb("pos", [P, TT * TOPK])
            far = sb("far", [P, TT * TOPK])
            slot = sb("slot", [P, TT * TOPK])
            slot_i = sb("slot_i", [P, TT * TOPK], U32)
            blank_row = rowx[:, 0, :]

            block = first.enter_context(nc.Block())

            @block.sync
            def _(sp):
                sp.dma_start(inw[:, :, :], in_w).then_inc(inner_in, 16)
                sp.dma_start(ctxT[:, :, :], ctx_t[0]).then_inc(ctx_in, 16)
                sp.dma_start(chn_w[:, :, :], chan).then_inc(inner_in, 16)
                sp.dma_start(xpw[:, :, :], xp_w).then_inc(inner_in, 16)
                sp.dma_start(dtw[:, :], dtp_w).then_inc(inner_in, 16)
                sp.dma_start(cb16[:, :], const_b).then_inc(inner_in, 16)
                sp.dma_start(cf[:, :], const_f).then_inc(weights_in, 16)
                sp.dma_start(lat, lat_w).then_inc(weights_in, 16)
                sp.dma_start(cmp_w[:, :], comp_w).then_inc(weights_in, 16)
                sp.dma_start(wqk[:, :], qk_w).then_inc(weights_in, 16)
                sp.dma_start(gw[:, :, :], gate_w).then_inc(weights_in, 16)
                sp.dma_start(tokb[:, :], token_b).then_inc(weights_in, 16)

                def load_ctx(b):
                    sp.wait_ge(*done("ln0_T", b - 1, TT - 1))
                    sp.dma_start(ctxT[:, :, :], ctx_t[b]).then_inc(ctx_in, 16)

                def load_tile(b, t):
                    if t >= 2:
                        sp.wait_ge(*done("ln0_T", b, t - 2))
                    else:
                        sp.wait_ge(*done("in_proj", b, CH - 1))
                    sp.dma_start(xr[:, t % 2, :], x[b, t]).then_inc(x_tile_in[t % 2], 16)

                def load_batch(b):
                    if b >= 2:
                        sp.wait_ge(stored, 16 * TT * (b - 1))
                    sp.dma_start(base[:, b % 2, :, :], x[b].rearrange("t p d -> p t d")).then_inc(x_batch_in[b % 2], 16)

                def load_shared(b):
                    for f in range(KF):
                        if f >= 2:
                            sp.wait_ge(*done("ffn_up", b, f - 2))
                        elif b:
                            sp.wait_ge(*done("ffn_down", b - 1, TT - 1))
                        sp.dma_start(shw[:, f % 2, :, :], shared_w[:, f * 2 * KD * P:(f + 1) * 2 * KD * P].rearrange(
                            "p (w n) -> p w n", w=2)).then_inc(shared_in[f % 2], 16)

                def load_down(b):
                    for i in range(2):
                        sp.wait_ge(*done("ffn_up", b, KF - 2 + i))
                        half = slice(i * KF // 2 * D, (i + 1) * KF // 2 * D)
                        sp.dma_start(sh_down[:, half], shared_w[:, KF * 2 * KD * P:][:, half]).then_inc(down_in[i], 16)

                def store(b):
                    for t in range(TT):
                        sp.wait_ge(*done("ffn_add", b, t))
                        sp.dma_start(out[(b * TT + t) * P:(b * TT + t + 1) * P, :],
                                     base[:, b % 2, t, :]).then_inc(stored, 16)

                for phase in range(-1, B + 1):
                    b = phase + 1
                    if b < B:
                        for t in range(TT):
                            load_tile(b, t)
                            if phase >= 1 and t == 1:
                                load_shared(phase - 1)
                            if phase >= 1 and t == 2:
                                load_down(phase - 1)
                    elif phase >= 1:
                        load_shared(phase - 1)
                        load_down(phase - 1)
                    if phase >= 1:
                        store(phase - 1)
                    if b < B:
                        load_batch(b)
                    if b == 0:
                        sp.wait_ge(setup, 2)
                        sp.dma_start(rows_dram.rearrange("(e p) r -> p e r", p=CAP),
                                     rowx[:, 0:1, :].to_broadcast([P, E, ROW])).then_inc(rows_zeroed, 16)
                        sp.dma_start(out[B * T:B * T + P, :], rowx[:, 1, 0:D]).then_inc(rows_zeroed, 16)
                    if b + 1 < B:
                        load_ctx(b + 1)
                sp.wait_ge(stored, 16 * TT * B)

            @block.gpsimd
            def _(pool):
                own = [0]

                def settle(ins):
                    own[0] += 1
                    ins.then_inc(pool_own, 1)
                    pool.wait_ge(pool_own, own[0])

                settle(nc.gpsimd.memset(mhalf[:, :], -0.5))
                settle(nc.gpsimd.memset(upad[:, 0:3], 0.0))
                settle(nc.gpsimd.memset(gs8[:, :, :], NEG))
                settle(nc.gpsimd.memset(seen[:, :], 0.0))
                nc.gpsimd.memset(rowx[:, :, :], 0.0).then_inc(setup, 1)
                pool.wait_ge(setup, 1)
                pool.wait_ge(weights_in, 16 * 6)
                nc.gpsimd.tensor_copy(blank_row[:, ID_AT:ID_AT + 1], cf[:, at + 2 * E:at + 2 * E + 1]).then_inc(setup, 1)
                def rstd(rs, nbias, mv, task):
                    mean, var = mv[:, :, 0], mv[:, :, 1]
                    nc.gpsimd.tensor_scalar(nbias, mean, -1.0, None, ALU.mult)
                    settle(nc.gpsimd.tensor_scalar(rs, var, EPS, None, ALU.add))
                    settle(nc.gpsimd.tensor_tensor(rs, rs, mhalf[:, 0:rs.shape[-1]], ALU.pow))
                    nc.gpsimd.tensor_tensor(nbias, nbias, rs, ALU.mult).then_inc(S[task], 1)

                def e_rest(b, c):
                    pool.wait_ge(*done("e_round", b, c))
                    nc.gpsimd.tensor_tensor(c4[:, c, :], e4[:, c, :], c4[:, c, :], ALU.subtract).then_inc(S["e_rest"], 1)

                def log1p(b, c):
                    pool.wait_ge(*done("ln", b))
                    pool.wait_ge(*done("e_rest", b, CH - 1))
                    nc.gpsimd.tensor_tensor(c4[:, c, :], e4[:, c, :], c4[:, c, :], ALU.add).then_inc(S["log1p"], 1)

                def ln0_rstd(b, t):
                    pool.wait_ge(*done("ln0_aggr", b, t))
                    if b:
                        pool.wait_ge(*done("ln0_norm", b - 1, t))
                    rstd(rs0[:, t:t + 1], nb0[:, t:t + 1], mv0[:, t:t + 1, :], "ln0_rstd")

                def c_rstd(b, i):
                    pool.wait_ge(*done("c_aggr", b))
                    settle(nc.gpsimd.tensor_scalar(rsc[:, :], mvc[:, :, 1], EPS, None, ALU.add))
                    nc.gpsimd.tensor_tensor(rsc[:, :], rsc[:, :], mhalf[:, :], ALU.pow).then_inc(S["c_rstd"], 1)

                def x1_rstd(b, i):
                    pool.wait_ge(*done("x1_aggr", b, TT - 1))
                    if b:
                        pool.wait_ge(*done("g_norm", b - 1, CH - 1))
                    rstd(rs1[:, :], nb1[:, :], mv1[:, :, :], "x1_rstd")

                def ln2_rstd(b, i):
                    pool.wait_ge(*done("ln2_aggr", b, TT - 1))
                    if b:
                        pool.wait_ge(*done("ln2_norm", b - 1, TT - 1))
                    rstd(rs2[:, :], nb2[:, :], mv2[:, :, :], "ln2_rstd")

                def x_bias(b, t):
                    pool.wait_ge(x_batch_in[b % 2], 16 * (b // 2 + 1))
                    h = base[:, b % 2, t, :]
                    nc.gpsimd.tensor_tensor(h, h, bias_out, ALU.add).then_inc(S["x_bias"], 1)

                def scatter(b, j):
                    pool.wait_ge(*done("slots", b, N_SLOTS - 1))
                    pool.wait_ge(*done("route", b, N_ROUTE - 1))
                    pool.wait_ge(*done("ln2_norm", b, TT - 1))
                    if b == 0 and j == 0:
                        pool.wait_ge(rows_zeroed, 32)
                    nc.gpsimd.indirect_dma_start(
                        out=rows_dram, out_offset=bass.IndirectOffsetOnAxis(ap=slot_i[:, j:j + 1], axis=0),
                        in_=rowx[:, j // TOPK, :], in_offset=None, bounds_check=E * CAP - 1,
                        oob_is_err=False).then_inc(scattered, 16)

                tasks = dict(e_rest=e_rest, log1p=log1p, x_bias=x_bias, ln0_rstd=ln0_rstd, c_rstd=c_rstd,
                             x1_rstd=x1_rstd, ln2_rstd=ln2_rstd, scatter=scatter)
                for phase in range(-1, B + 2):
                    for step in range(STEPS):
                        k = phase * STEPS + step + AHEAD_POOL
                        if 0 <= k < NK:
                            b, c, n = k // STEPS, k % STEPS // NS, k % NS
                            if k >= N_DBU:
                                pool.wait_ge(S["scan"], k - N_DBU + 1)
                            if n == 0:
                                pool.wait_ge(*done("dtu", b, c))
                            pool.wait_ge(*done("b_copy", b, n))
                            nc.gpsimd.tensor_tensor(scan_in[:, k % N_DBU, :], dtu[:, c, :], b_all[:, n, :],
                                                    ALU.mult).then_inc(S["scan_in"], 1)
                        for task, b, i in side_work("pool", phase, step):
                            tasks[task](b, i)
                pool.wait_ge(scattered, 16 * TT * TOPK * B)

            @block.scalar
            def _(act):
                own = [0]

                def settle(ins):
                    own[0] += 1
                    ins.then_inc(act_own, 1)
                    act.wait_ge(act_own, own[0])

                def bank(task, b, i=0):
                    act.wait_ge(*done(task, b, i))
                    return banks[BANK[(task, i)] if (task, i) in BANK else BANK[(task + "_lo", i)]]

                act.wait_ge(inner_in, 16 * 5)
                act.wait_ge(setup, 1)
                settle(nc.scalar.activation(a_neg[:, :, :], a_log, ACT.Exp))
                settle(nc.scalar.mul(a_neg[:, :, :], a_neg[:, :, :], -1.0))

                def fold():
                    act.wait_ge(weights_in, 16 * 6)
                    act.wait_ge(weff_psum, 1)
                    nc.scalar.copy(weff[:, :, :], banks[0][:, 0:KD * DC].rearrange("p (k c) -> p k c", c=DC)).then_inc(folded, 1)
                    act.wait_ge(weff_psum, 2)
                    nc.scalar.copy(wout[:, :], banks[2][0:DC, :]).then_inc(folded, 1)
                    act.wait_ge(folded, 2)

                def u_copy(b, c):
                    if b * CH + c:
                        act.wait_ge(S["conv"], 3 * (b * CH + c))
                    nc.scalar.copy(upad[:, 3:], bank("in_proj", b, c)[:, :]).then_inc(S["u_copy"], 1)

                def normed(to, src, nbias, rs, task):
                    nc.scalar.activation(to, src, ACT.Identity, scale=rs, bias=nbias).then_inc(S[task], 1)

                def conv_first(b, c):
                    act.wait_ge(*done("u_copy", b, c))
                    if b >= 2:
                        act.wait_ge(*done("y_sum", b - 2, c))
                        act.wait_ge(*done("dtu", b - 2, c))
                        act.wait_ge(*done("x_proj", b - 2))
                    nc.scalar.activation(u2[:, b % 2, c, :], upad[:, 0:T], ACT.Identity, scale=conv_w(c, 0),
                                         bias=conv_b(c)).then_inc(S["conv_first"], 1)

                def ln0_norm(b, t):
                    act.wait_ge(*done("ln0_rstd", b, t))
                    normed(xr[:, t % 2, :], xr[:, t % 2, :], nb0[:, t:t + 1], rs0[:, t:t + 1], "ln0_norm")

                def g_norm(b, c):
                    act.wait_ge(*done("x1_rstd", b))
                    if b:
                        act.wait_ge(*done("g_mul", b - 1, c))
                    else:
                        act.wait_ge(weff_psum, 2)
                    normed(gx[:, c, :], base[:, b % 2, c, :], nb1[:, c:c + 1], rs1[:, c:c + 1], "g_norm")

                def ln2_norm(b, t):
                    act.wait_ge(*done("ln2_rstd", b))
                    if t == 0:
                        act.wait_ge(scattered, 16 * TT * TOPK * b) if b else act.wait_ge(rows_zeroed, 32)
                    normed(rowx[:, t, 0:D], base[:, b % 2, t, :], nb2[:, t:t + 1], rs2[:, t:t + 1], "ln2_norm")

                def conv_tanh(b, c):
                    act.wait_ge(*done("conv", b, 3 * c + 2))
                    if b * CH + c:
                        act.wait_ge(S["u_gate"], b * CH + c)
                    nc.scalar.activation(cth[:, :], u2[:, b % 2, c, :], ACT.Tanh, scale=0.5).then_inc(S["conv_tanh"], 1)

                def x_copy(b, i):
                    if b:
                        act.wait_ge(*done("dt_proj", b - 1, CH - 1))
                        act.wait_ge(*done("split", b - 1, N_SPLIT - 1))
                    nc.scalar.mul(xd[:, :], bank("x_proj", b)[0:DC, :], 0.5).then_inc(S["x_copy"], 1)

                def dt_exp(b, c):
                    z = bank("dt_proj", b, c)
                    m = b * CH + c
                    if m >= N_DT:
                        act.wait_ge(S["decay"], NS * (m - N_DT + 1))
                        act.wait_ge(S["dtu"], m - N_DT + 1)
                    if c == 0:
                        act.wait_ge(*done("split", b, N_SPLIT - 1))
                    nc.scalar.activation(dt_of(b, c), z[:, :], ACT.Identity, bias=dt_b(c))
                    settle(nc.scalar.activation(e4[:, c, :], z[:, :], ACT.Abs, bias=dt_b(c)))
                    nc.scalar.activation(e4[:, c, :], e4[:, c, :], ACT.Exp, scale=-1.0).then_inc(S["dt_exp"], 1)

                def ln(b, i):
                    act.wait_ge(*done("e_rest", b, CH - 1))
                    nc.scalar.activation(e4[:, :, :], e4[:, :, :], ACT.Ln, bias=1.0).then_inc(S["ln"], 1)

                def b_copy(b, n):
                    if b:
                        act.wait_ge(S["scan_in"], b * STEPS - NS + n + 1)
                    nc.scalar.copy(b_all[:, n, :], bank("b_bcast", b, n)[:, :]).then_inc(S["b_copy"], 1)

                def ln0_T_copy(b, t):
                    if b >= 2:
                        act.wait_ge(*done("ffn_up", b - 2, KF - 1))
                    elif b == 1:
                        act.wait_ge(*done("c_proj", 0))
                    src = bank("ln0_T", b, t)[:, :].rearrange("p (k c) -> p k c", c=P)
                    nc.scalar.copy(xT[:, :, t * P:(t + 1) * P], src).then_inc(S["ln0_T_copy"], 1)

                def ln2_T_copy(b, t):
                    act.wait_ge(*done("c_proj", min(b + 1, B - 1)))
                    if b == B - 1:
                        act.wait_ge(*done("ffn_up", b - 1, KF - 1))
                    src = bank("ln2_T", b, t)[:, :].rearrange("p (k c) -> p k c", c=P)
                    nc.scalar.copy(xT[:, :, t * P:(t + 1) * P], src).then_inc(S["ln2_T_copy"], 1)

                def c_copy(b, i):
                    if b:
                        act.wait_ge(*done("c_T", b - 1))
                    act.wait_ge(*done("dt", b, CH - 1))
                    nc.scalar.copy(cn, bank("c_proj", b)[:, 0:TT * DC].rearrange("p (t c) -> p t c", c=DC)).then_inc(S["c_copy"], 1)

                def c_affine(b, i):
                    if b:
                        act.wait_ge(*done("v", b - 1))
                    act.wait_ge(*done("dt", b, CH - 1))
                    nc.scalar.activation(chT, bank("c_T", b)[0:DC, :], ACT.Identity,
                                         scale=cmp_w[0:DC, 2 * DC:2 * DC + 1], bias=cmp_w[0:DC, 2 * DC + 1:2 * DC + 2]).then_inc(S["c_affine"], 1)

                def v_copy(b, i):
                    act.wait_ge(*done("dt", b, CH - 1))
                    nc.scalar.copy(v_sb, bank("v", b)[:, 0:TT * DC].rearrange("p (t c) -> p t c", c=DC)).then_inc(S["v_copy"], 1)

                def p_exp(b, t):
                    act.wait_ge(*done("score_neg", b, t))
                    if t >= 2:
                        act.wait_ge(*done("p_T", b, t - 2))
                    elif b >= 2:
                        act.wait_ge(*done("ffn_down", b - 2, TT - 1))
                    w = (t + 1) * P
                    nc.scalar.activation(probs[:, t % 2, 0:w], bank("score", b, t)[:, 0:w], ACT.Exp, scale=DC ** -0.5,
                                         bias=nmax[:, t:t + 1], accum_out=psums[:, t:t + 1]).then_inc(S["p_exp"], 1)

                def p_T_copy(b, t):
                    if t >= 2:
                        act.wait_ge(*done("pv", b, t - 2))
                    w = (t + 1) * P
                    nc.scalar.copy(probsT[:, t % 2, 0:w], bank("p_T", b, t)[:, 0:w]).then_inc(S["p_T_copy"], 1)

                def pv_copy(b, t):
                    nc.scalar.copy(oT[:, t * P:(t + 1) * P], bank("pv", b, t)[0:DC, 0:P]).then_inc(S["pv_copy"], 1)

                def g_tanh(b, c):
                    act.wait_ge(*done("g_norm", b, c))
                    if b * CH + c:
                        act.wait_ge(S["y_gate"], b * CH + c)
                    nc.scalar.activation(gt[:, :], gx[:, c, :], ACT.Tanh, scale=0.5).then_inc(S["g_tanh"], 1)

                def logits_tanh(b, i):
                    if b:
                        act.wait_ge(*done("route", b - 1, N_ROUTE - 1))
                    src = bank("logits", b)[:, 0:TT * E].rearrange("p (t e) -> p t e", e=E)
                    nc.scalar.activation(score[:, :, :], src, ACT.Tanh, scale=0.5).then_inc(S["logits_tanh"], 1)

                def ffn_tanh(b, f):
                    if b * KF + f >= 1:
                        act.wait_ge(S["ffn_h"], b * KF + f)
                    nc.scalar.activation(fth[:, :], bank("ffn_gate", b, f)[:, :], ACT.Tanh, scale=0.5).then_inc(S["ffn_tanh"], 1)

                tasks = dict(u_copy=u_copy, conv_first=conv_first, ln0_norm=ln0_norm, g_norm=g_norm, ln2_norm=ln2_norm,
                             conv_tanh=conv_tanh, x_copy=x_copy, dt_exp=dt_exp, ln=ln, b_copy=b_copy,
                             ln0_T_copy=ln0_T_copy, ln2_T_copy=ln2_T_copy, c_copy=c_copy, c_affine=c_affine, v_copy=v_copy, p_exp=p_exp,
                             p_T_copy=p_T_copy, pv_copy=pv_copy, g_tanh=g_tanh, logits_tanh=logits_tanh, ffn_tanh=ffn_tanh)
                for phase in range(-1, B + 2):
                    for step in range(STEPS):
                        if (phase, step) == FOLD_AT:
                            fold()
                        k = phase * STEPS + step + AHEAD_ACT
                        if 0 <= k < NK:
                            b, c, n = k // STEPS, k % STEPS // NS, k % NS
                            if k >= N_DA:
                                act.wait_ge(S["scan"], k - N_DA + 1)
                            if n == 0:
                                act.wait_ge(*done("dt", b, c))
                            nc.scalar.activation(decay_ps[k % N_DA][:, :], dt_of(b, c), ACT.Exp,
                                                 scale=a_neg[:, c, n:n + 1]).then_inc(S["decay"], 1)
                        for task, b, i in side_work("act", phase, step):
                            tasks[task](b, i)

            @block.vector
            def _(dve):
                own = [0]

                def settle(ins):
                    own[0] += 1
                    ins.then_inc(dve_own, 1)
                    dve.wait_ge(dve_own, own[0])

                def bank(task, b, i=0):
                    dve.wait_ge(*done(task, b, i))
                    return banks[BANK[(task, i)] if (task, i) in BANK else BANK[(task + "_lo", i)]]

                V = nc.vector
                dve.wait_ge(inner_in, 16 * 5)
                dve.wait_ge(setup, 1)
                for c in range(CH):
                    settle(V.tensor_scalar(skip_d(c), skip_d(c), 0.5, None, ALU.mult))

                def fold():
                    dve.wait_ge(weights_in, 16 * 6)
                    dve.wait_ge(setup, 2)
                    V.tensor_tensor(lat[:, D:2 * D], lat[:, 0:D], lat[:, D:2 * D], ALU.add).then_inc(lat_summed, 1)

                def conv(b, i):
                    c, j = i // 3, i % 3 + 1
                    if j == 1:
                        dve.wait_ge(*done("conv_first", b, c))
                    else:
                        dve.wait_ge(*done("conv", b, i - 1))
                    o = u2[:, b % 2, c, :]
                    V.scalar_tensor_tensor(o, upad[:, j:j + T], conv_w(c, j), o, ALU.mult, ALU.add).then_inc(S["conv"], 1)

                def u_gate(b, c):
                    dve.wait_ge(*done("conv_tanh", b, c))
                    u = u2[:, b % 2, c, :]
                    V.scalar_tensor_tensor(u, cth[:, :], 1.0, u, ALU.add, ALU.mult).then_inc(S["u_gate"], 1)

                def split(b, i):
                    parts, bc, r, mid = bc_parts[:, b % 2, :], xd[32:64, :], bc_rest[32:64, :], bc_mid[32:64, :]
                    if i == 0:
                        dve.wait_ge(*done("x_copy", b))
                        if b:
                            dve.wait_ge(*done("score", b - 1, TT - 1))
                        if b >= 2:
                            dve.wait_ge(S["c_bcast"], (b - 1) * STEPS)
                            dve.wait_ge(*done("b_bcast", b - 2, NS - 1))
                        ins = V.tensor_copy(parts[32:64, :], bc)
                    else:
                        dve.wait_ge(*done("split", b, i - 1))
                    if i == 1:
                        ins = V.tensor_tensor(r, bc, parts[32:64, :], ALU.subtract)
                    elif i == 2:
                        V.tensor_copy(parts[0:32, :], r)
                        ins = V.tensor_copy(mid, r)
                    elif i == 3:
                        ins = V.tensor_tensor(parts[64:96, :], r, mid, ALU.subtract)
                    ins.then_inc(S["split"], 1)

                def e_round(b, c):
                    dve.wait_ge(*done("dt_exp", b, c))
                    if b and c == 0:
                        dve.wait_ge(*done("attn_out", b - 1, TT - 1))
                    V.tensor_scalar(c4[:, c, :], e4[:, c, :], 1.0, -1.0, ALU.add, ALU.add).then_inc(S["e_round"], 1)

                def dt(b, c):
                    dve.wait_ge(*done("log1p", b, c))
                    V.scalar_tensor_tensor(dt_of(b, c), dt_of(b, c), 0.0, c4[:, c, :], ALU.max, ALU.add).then_inc(S["dt"], 1)

                def dtu_(b, c):
                    dve.wait_ge(*done("dt", b, c))
                    if b:
                        dve.wait_ge(S["scan_in"], (b - 1) * STEPS + (c + 1) * NS)
                    V.scalar_tensor_tensor(dtu[:, c, :], u2[:, b % 2, c, :], 0.5, dt_of(b, c), ALU.mult, ALU.mult).then_inc(S["dtu"], 1)

                def stats(kind, wait, source, mv, name):
                    def first(b, t):
                        wait(b, t)
                        if b:
                            dve.wait_ge(*done(f"{name}_aggr", b - 1, t))
                        V.bn_stats(st6[:, kind, t, :], source(b, t)).then_inc(S[f"{name}_stats"], 1)

                    def second(b, t):
                        dve.wait_ge(*done(f"{name}_stats", b, t))
                        if b:
                            dve.wait_ge(*done(f"{name}_rstd", b - 1, t if name == "ln0" else 0))
                        V.bn_aggr(mv[:, t, :], st6[:, kind, t, :]).then_inc(S[f"{name}_aggr"], 1)
                    return first, second

                ln0_stats, ln0_aggr = stats(0, lambda b, t: dve.wait_ge(x_tile_in[t % 2], 16 * ((b * TT + t) // 2 + 1)),
                                            lambda b, t: xr[:, t % 2, :], mv0, "ln0")
                x1_stats, x1_aggr = stats(1, lambda b, t: dve.wait_ge(*done("x1", b, t)),
                                          lambda b, t: base[:, b % 2, t, :], mv1, "x1")
                ln2_stats, ln2_aggr = stats(2, lambda b, t: dve.wait_ge(*done("y_add", b, CH - 1)),
                                            lambda b, t: base[:, b % 2, t, :], mv2, "ln2")

                def c_stats(b, i):
                    dve.wait_ge(*done("c_copy", b))
                    if b:
                        dve.wait_ge(*done("c_aggr", b - 1))
                    for t in range(TT):
                        last = V.bn_stats(st6[:, 3, t, :], cn[:, t, :])
                    last.then_inc(S["c_stats"], 1)

                def c_aggr(b, i):
                    dve.wait_ge(*done("c_stats", b))
                    if b:
                        dve.wait_ge(*done("c_norm", b - 1))
                    for t in range(TT):
                        last = V.bn_aggr(mvc[:, t, :], st6[:, 3, t, :])
                    last.then_inc(S["c_aggr"], 1)

                def c_norm(b, i):
                    dve.wait_ge(*done("c_rstd", b))
                    for t in range(TT):
                        last = V.tensor_scalar(cn[:, t, :], cn[:, t, :], mvc[:, t, 0:1], rsc[:, t:t + 1],
                                               ALU.subtract, ALU.mult)
                    last.then_inc(S["c_norm"], 1)

                def rope_cos(b, i):
                    dve.wait_ge(*done("log1p", b, CH - 1))
                    V.tensor_tensor(r_cos, bank("qk", b)[:, :], cos, ALU.mult).then_inc(S["rope_cos"], 1)

                def rope_sin(b, i):
                    V.tensor_tensor(r_sin, bank("qk_rolled", b)[:, :], sin, ALU.mult).then_inc(S["rope_sin"], 1)

                def rope_add(b, i):
                    dve.wait_ge(*done("rope_sin", b))
                    to, at_ = ((qT, 0), (kT, DC))[i]
                    V.tensor_tensor(to, r_cos[at_:at_ + DC, :], r_sin[at_:at_ + DC, :], ALU.add).then_inc(S["rope_add"], 1)

                def score_mask(b, t):
                    ps = bank("score", b, t)[:, t * P:(t + 1) * P]
                    V.tensor_tensor(ps, ps, cmask, ALU.add).then_inc(S["score_mask"], 1)

                def score_max(b, t):
                    dve.wait_ge(*done("score_mask", b, t))
                    V.tensor_reduce(nmax[:, t:t + 1], bank("score", b, t)[:, 0:(t + 1) * P], AX_X, ALU.max).then_inc(S["score_max"], 1)

                def score_neg(b, t):
                    dve.wait_ge(*done("score_max", b, t))
                    V.tensor_scalar(nmax[:, t:t + 1], nmax[:, t:t + 1], -DC ** -0.5, None, ALU.mult).then_inc(S["score_neg"], 1)

                def p_recip(b, t):
                    dve.wait_ge(*done("p_exp", b, t))
                    V.reciprocal(prec[:, t:t + 1], psums[:, t:t + 1]).then_inc(S["p_recip"], 1)

                def x1(b, t):
                    dve.wait_ge(*done("x_bias", b, t))
                    dve.wait_ge(*done("p_recip", b, t))
                    h = base[:, b % 2, t, :]
                    V.scalar_tensor_tensor(h, bank("attn_out", b, t)[:, :], prec[:, t:t + 1], h, ALU.mult, ALU.add).then_inc(S["x1"], 1)

                def g_mul(b, c):
                    dve.wait_ge(*done("g_tanh", b, c))
                    V.scalar_tensor_tensor(gt[:, :], gt[:, :], 1.0, gx[:, c, :], ALU.add, ALU.mult).then_inc(S["g_mul"], 1)

                def y_sum(b, c):
                    dve.wait_ge(S["state_sum"], b * STEPS + (c + 1) * NS)
                    if b * CH + c:
                        dve.wait_ge(S["y_T"], b * CH + c)
                    V.scalar_tensor_tensor(ybuf[:, :], u2[:, b % 2, c, :], skip_d(c), y_ps[:, :], ALU.mult, ALU.add).then_inc(S["y_sum"], 1)

                def y_gate(b, c):
                    dve.wait_ge(*done("y_sum", b, c))
                    dve.wait_ge(*done("g_mul", b, c))
                    V.scalar_tensor_tensor(ybuf[:, :], ybuf[:, :], 0.5, gt[:, :], ALU.mult, ALU.mult).then_inc(S["y_gate"], 1)

                def y_add(b, c):
                    dve.wait_ge(*done("g_norm", b, CH - 1))
                    h = base[:, b % 2, :, c * P:(c + 1) * P]
                    src = bank("y_T", b, c)[:, :].rearrange("p (t c) -> p t c", c=P)
                    V.tensor_tensor(h, h, src, ALU.add).then_inc(S["y_add"], 1)

                every_tile = lambda v: v.rearrange("p (a e) -> p a e", a=1).to_broadcast([P, TT, E])
                groups = every_tile(iota_g)
                eif_v = eif[:, :].rearrange("p (t k) -> p t k", k=TOPK)
                wraw_v = wraw[:, :].rearrange("p (t k) -> p t k", k=TOPK)
                of_tile = lambda v, t: v[:, t * TOPK:(t + 1) * TOPK, :]

                def route(b, i):
                    dve.wait_ge(*(done("route", b, i - 1) if i else done("logits_tanh", b)))
                    if i == 0:
                        if b:
                            dve.wait_ge(*done("slots", b - 1, N_SLOTS - 1))
                        m = V.tensor_scalar(score[:, :, :], score[:, :, :], 0.5, 0.5, ALU.mult, ALU.add)
                    elif i == 1:
                        m = V.tensor_tensor(score_b[:, :, :], score[:, :, :], every_tile(bias_gate), ALU.add)
                    elif i == 2:
                        for j in range(TT * G):
                            m = V.max(m8[:, j, :], score_b[:, j // G, (j % G) * 8:(j % G) * 8 + 8])
                    elif i == 3:
                        m = V.tensor_tensor(gs8[:, :, 0:G], m8[:, :, 0].rearrange("p (t g) -> p t g", g=G),
                                            m8[:, :, 1].rearrange("p (t g) -> p t g", g=G), ALU.add)
                    elif i == 4:
                        for t in range(TT):
                            m = V.max(g8[:, t, :], gs8[:, t, :])
                    elif i == 5:
                        for t in range(TT):
                            m = V.max_index(gi[:, t, :], g8[:, t, :], gs8[:, t, :])
                    elif i == 6:
                        m = V.tensor_copy(gif[:, :, :], gi[:, :, 0:2])
                    elif i == 7:
                        V.tensor_tensor(kept[:, :, :], groups, gif[:, :, 0:1].to_broadcast([P, TT, E]), ALU.is_equal)
                        m = V.tensor_tensor(kept2[:, :, :], groups, gif[:, :, 1:2].to_broadcast([P, TT, E]), ALU.is_equal)
                    elif i == 8:
                        m = V.tensor_tensor(kept[:, :, :], kept[:, :, :], kept2[:, :, :], ALU.add)
                    elif i == 9:
                        m = V.tensor_tensor(kept[:, :, :], kept[:, :, :], score_b[:, :, :], ALU.mult)
                    elif i == 10:
                        m = V.tensor_scalar(kept[:, :, :], kept[:, :, :], 0.0, None, ALU.add)
                    elif i == 11:
                        for t in range(TT):
                            m = V.max(t8[:, t, :], kept[:, t, :])
                    elif i == 12:
                        for t in range(TT):
                            m = V.max_index(ti[:, t, :], t8[:, t, :], kept[:, t, :])
                    elif i == 13:
                        m = V.tensor_copy(eif_v, ti[:, :, 0:TOPK])
                    elif i == 14:
                        m = V.tensor_tensor(hot[:, :, :], iota_e.rearrange("p (a e) -> p a e", a=1).to_broadcast([P, TT * TOPK, E]),
                                            eif[:, :].rearrange("p (j a) -> p j a", a=1).to_broadcast([P, TT * TOPK, E]), ALU.is_equal)
                    elif i == CHOSEN:
                        with nc.allow_low_precision(reason="zeros and ones are exact in bfloat16"):
                            m = V.tensor_reduce(chosen[:, :, :], hot[:, :, :].rearrange("p (t k) e -> p t e k", k=TOPK), AX_X, ALU.add)
                    elif i == 16:
                        for t in range(TT):
                            m = V.tensor_tensor(of_tile(prod, t), of_tile(hot, t), score[:, t:t + 1, :].to_broadcast([P, TOPK, E]), ALU.mult)
                    elif i == SCORED:
                        m = V.tensor_reduce(wraw[:, :], prod[:, :, :], AX_X, ALU.add)
                    elif i == 18:
                        m = V.tensor_reduce(wsum[:, :], wraw_v, AX_X, ALU.add)
                    elif i == 19:
                        settle(V.tensor_scalar(wsum[:, :], wsum[:, :], 1e-20, None, ALU.add))
                        settle(V.reciprocal(wsum[:, :], wsum[:, :]))
                        if b:
                            dve.wait_ge(scattered, 16 * TT * TOPK * b)
                        V.tensor_copy(rowx[:, :, E_AT:E_AT + TOPK], eif_v)
                        V.tensor_copy(rowx[:, :, ID_AT:ID_AT + 1],
                                      tok_id[:, b * TT:(b + 1) * TT].rearrange("p (t a) -> p t a", a=1))
                        m = V.tensor_tensor(rowx[:, :, W_AT:W_AT + TOPK], wraw_v,
                                            wsum[:, :].rearrange("p (t a) -> p t a", a=1).to_broadcast([P, TT, TOPK]), ALU.mult)
                    m.then_inc(S["route"], 1)

                def slots(b, i):
                    if i:
                        dve.wait_ge(*done("slots", b, i - 1))
                    if i == 0:
                        cnt = bank("earlier", b)
                        dve.wait_ge(*done("route", b, SCORED))
                        for t in range(TT):
                            m = V.tensor_tensor(of_tile(prod, t), of_tile(hot, t),
                                                cnt[:, t * E:(t + 1) * E].rearrange("p (a e) -> p a e", a=1).to_broadcast([P, TOPK, E]), ALU.mult)
                    elif i == 1:
                        m = V.tensor_reduce(pos[:, :], prod[:, :, :], AX_X, ALU.add)
                    elif i == 2:
                        m = V.tensor_scalar(far[:, :], pos[:, :], float(CAP), FAR, ALU.is_ge, ALU.mult)
                    elif i == 3:
                        m = V.tensor_tensor(pos[:, :], pos[:, :], far[:, :], ALU.add)
                    elif i == 4:
                        m = V.scalar_tensor_tensor(slot[:, :], eif[:, :], float(CAP), pos[:, :], ALU.mult, ALU.add)
                    elif i == 5:
                        for t in range(TT):
                            settle(V.tensor_tensor(seen[:, :], seen[:, :], chosen[:, t, :], ALU.add))
                        if b:
                            dve.wait_ge(scattered, 16 * TT * TOPK * b)
                        m = V.tensor_copy(slot_i[:, :], slot[:, :])
                    m.then_inc(S["slots"], 1)

                def ffn_silu(b, f):
                    dve.wait_ge(*done("ffn_tanh", b, f))
                    V.scalar_tensor_tensor(fth[:, :], fth[:, :], 1.0, bank("ffn_gate", b, f)[:, :], ALU.add, ALU.mult).then_inc(S["ffn_silu"], 1)

                def ffn_h(b, f):
                    dve.wait_ge(*done("ffn_silu", b, f))
                    if f == 0:
                        dve.wait_ge(*done("pv", min(b + 1, B - 1), TT - 1))
                        if b:
                            dve.wait_ge(*done("ffn_down", b - 1, TT - 1))
                    V.scalar_tensor_tensor(hT[:, f, :], fth[:, :], 0.5, bank("ffn_up", b, f)[:, :], ALU.mult, ALU.mult).then_inc(S["ffn_h"], 1)

                def ffn_add(b, t):
                    h = base[:, b % 2, t, :]
                    V.tensor_tensor(h, h, bank("ffn_down", b, t)[:, :], ALU.add).then_inc(S["ffn_add"], 1)

                tasks = dict(dtu=dtu_, conv=conv, u_gate=u_gate, split=split, e_round=e_round, dt=dt,
                             ln0_stats=ln0_stats, ln0_aggr=ln0_aggr, c_stats=c_stats, c_aggr=c_aggr,
                             c_norm=c_norm, rope_cos=rope_cos, rope_sin=rope_sin, rope_add=rope_add,
                             score_mask=score_mask, score_max=score_max, score_neg=score_neg, p_recip=p_recip,
                             x1=x1, x1_stats=x1_stats, x1_aggr=x1_aggr, g_mul=g_mul, y_sum=y_sum,
                             y_gate=y_gate, y_add=y_add, ln2_stats=ln2_stats, ln2_aggr=ln2_aggr, route=route,
                             slots=slots, ffn_silu=ffn_silu, ffn_h=ffn_h, ffn_add=ffn_add)

                def times_c(k):
                    dve.wait_ge(S["scan"], k + 1)
                    dve.wait_ge(S["c_bcast"], k + 1)
                    if k >= N_HC:
                        dve.wait_ge(S["state_sum"], k - N_HC + 1)
                    V.tensor_tensor(state_c[:, k % N_HC, :], state[:, k % N_H, :], cb_ps[k % N_CB][:, :], ALU.mult).then_inc(S["times_c"], 1)

                for phase in range(-1, B + 2):
                    for step in range(STEPS):
                        if (phase, step) == FOLD_AT:
                            fold()
                        k = phase * STEPS + step
                        if 0 <= phase < B:
                            dve.wait_ge(S["decay"], k + 1)
                            dve.wait_ge(S["scan_in"], k + 1)
                            if k >= N_H:
                                dve.wait_ge(S["times_c"], k - N_H + 1)
                            V.tensor_tensor_scan(state[:, k % N_H, :], decay_ps[k % N_DA][:, :], scan_in[:, k % N_DBU, :],
                                                 0.0, ALU.mult, ALU.add).then_inc(S["scan"], 1)
                        for task, b, i in side_work("dve", phase, step):
                            tasks[task](b, i)
                        if 0 <= k - 1 < NK:
                            times_c(k - 1)
                        for task, b, i in side_work("dve", phase, step + 0.5):
                            tasks[task](b, i)

            @block.tensor
            def _(pe):
                def bank(task, b, i=0):
                    prev = BEFORE[(task, b, i)]
                    if prev:
                        pe.wait_ge(*done(READER[prev[0]], *prev[1:]))
                    return banks[BANK[(task, i)]]

                MM = nc.tensor.matmul
                pe.wait_ge(inner_in, 16 * 5)

                def fold():
                    pe.wait_ge(weights_in, 16 * 6)
                    for k in range(KD):
                        last = MM(banks[0][:, k * DC:(k + 1) * DC], lat[:, k * P:(k + 1) * P], cmp_w[:, 0:DC], start=True, stop=True)
                    last.then_inc(weff_psum, 1)
                    pe.wait_ge(lat_summed, 1)
                    MM(banks[2][0:DC, :], cmp_w[:, DC:2 * DC], lat[:, D:2 * D], start=True, stop=True).then_inc(weff_psum, 1)

                def in_proj(b, c):
                    ps = bank("in_proj", b, c)
                    if c == 0:
                        pe.wait_ge(ctx_in, 16 * (b + 1))
                    for k in range(DCTX // P):
                        last = MM(ps[:, :], inw[:, k, c * P:(c + 1) * P], ctxT[:, k, :], start=(k == 0), stop=(k == DCTX // P - 1))
                    last.then_inc(S["in_proj"], 1)

                def x_proj(b, i):
                    ps = bank("x_proj", b)
                    pe.wait_ge(*done("u_gate", b, CH - 1))
                    for c in range(CH):
                        last = MM(ps[0:DC, :], xpw[:, c, :], u2[:, b % 2, c, :], start=(c == 0), stop=(c == CH - 1))
                    last.then_inc(S["x_proj"], 1)

                def dt_proj(b, c):
                    ps = bank("dt_proj", b, c)
                    pe.wait_ge(*done("x_copy", b))
                    MM(ps[:, :], dtw[:, c * P:(c + 1) * P], xd[0:RK, :], start=True, stop=True).then_inc(S["dt_proj"], 1)

                def b_bcast(b, n):
                    ps = bank("b_bcast", b, n)
                    pe.wait_ge(*done("split", b, N_SPLIT - 1))
                    MM(ps[:, :], pick[:, n:n + 1].to_broadcast([96, P]), bc_parts[:, b % 2, :], start=True, stop=True).then_inc(S["b_bcast"], 1)

                def turn(ps, src, task, n=KD):
                    for k in range(n):
                        last = nc.tensor.transpose(ps[:, k * P:(k + 1) * P], src(k), ident)
                    last.then_inc(S[task], 1)

                def ln0_T(b, t):
                    ps = bank("ln0_T", b, t)
                    pe.wait_ge(*done("ln0_norm", b, t))
                    turn(ps, lambda k: xr[:, t % 2, k * P:(k + 1) * P], "ln0_T")

                def c_proj(b, i):
                    ps = bank("c_proj", b)
                    pe.wait_ge(folded, 2)
                    pe.wait_ge(*done("ln0_T_copy", b, TT - 1))
                    for t in range(TT):
                        for k in range(KD):
                            last = MM(ps[:, t * DC:(t + 1) * DC], xT[:, k, t * P:(t + 1) * P], weff[:, k, :],
                                      start=(k == 0), stop=(k == KD - 1))
                    last.then_inc(S["c_proj"], 1)

                def c_T(b, i):
                    ps = bank("c_T", b)
                    pe.wait_ge(*done("c_norm", b))
                    for t in range(TT):
                        last = nc.tensor.transpose(ps[0:DC, t * P:(t + 1) * P], cn[:, t, :], ident)
                    last.then_inc(S["c_T"], 1)

                def qk(b, i):
                    ps = bank("qk", b)
                    pe.wait_ge(*done("c_affine", b))
                    MM(ps[:, :], wqk[:, 0:P], chT, start=True, stop=True).then_inc(S["qk"], 1)

                def qk_rolled(b, i):
                    ps = bank("qk_rolled", b)
                    MM(ps[:, :], wqk[:, P:2 * P], chT, start=True, stop=True).then_inc(S["qk_rolled"], 1)

                def v(b, i):
                    ps = bank("v", b)
                    for t in range(TT):
                        last = MM(ps[:, t * DC:(t + 1) * DC], chT[:, t * P:(t + 1) * P], wqk[:, 2 * P:2 * P + DC], start=True, stop=True)
                    last.then_inc(S["v"], 1)

                def score_(b, t):
                    ps = bank("score", b, t)
                    pe.wait_ge(*done("rope_add", b, 1))
                    MM(ps[:, 0:(t + 1) * P], qT[:, t * P:(t + 1) * P], kT[:, 0:(t + 1) * P], start=True, stop=True).then_inc(S["score"], 1)

                def p_T(b, t):
                    ps = bank("p_T", b, t)
                    pe.wait_ge(*done("p_exp", b, t))
                    turn(ps, lambda k: probs[:, t % 2, k * P:(k + 1) * P], "p_T", t + 1)

                def pv(b, t):
                    ps = bank("pv", b, t)
                    pe.wait_ge(*done("p_T_copy", b, t))
                    pe.wait_ge(*done("v_copy", b))
                    for j in range(t + 1):
                        last = MM(ps[0:DC, 0:P], v_sb[:, j, :], probsT[:, t % 2, j * P:(j + 1) * P], start=(j == 0), stop=(j == t))
                    last.then_inc(S["pv"], 1)

                def attn_out(b, t):
                    ps = bank("attn_out", b, t)
                    pe.wait_ge(*done("pv_copy", b, t))
                    MM(ps[:, :], oT[:, t * P:(t + 1) * P], wout[:, :], start=True, stop=True).then_inc(S["attn_out"], 1)

                def y_T(b, c):
                    ps = bank("y_T", b, c)
                    pe.wait_ge(*done("y_gate", b, c))
                    turn(ps, lambda t: ybuf[:, t * P:(t + 1) * P], "y_T", TT)

                def ln2_T(b, t):
                    ps = bank("ln2_T", b, t)
                    pe.wait_ge(*done("ln2_norm", b, t))
                    turn(ps, lambda k: rowx[:, t, k * P:(k + 1) * P], "ln2_T")

                def logits(b, i):
                    ps = bank("logits", b)
                    pe.wait_ge(*done("ln2_T_copy", b, TT - 1))
                    for t in range(TT):
                        for k in range(KD):
                            last = MM(ps[:, t * E:(t + 1) * E], xT[:, k, t * P:(t + 1) * P], gw[:, k, :],
                                      start=(k == 0), stop=(k == KD - 1))
                    last.then_inc(S["logits"], 1)

                def earlier(b, i):
                    ps = bank("earlier", b)
                    pe.wait_ge(*done("route", b, CHOSEN))
                    for t in range(TT):
                        o = ps[:, t * E:(t + 1) * E]
                        MM(o, before, chosen[:, t, :], start=True, stop=False)
                        for j in range(t):
                            MM(o, ones, chosen[:, j, :], start=False, stop=False)
                        last = MM(o, ones, seen[:, :], start=False, stop=True)
                    last.then_inc(S["earlier"], 1)

                def ffn_in(which, task, lo):
                    def run(b, f):
                        if lo:
                            bank(f"{task}_lo", b, f)
                            pe.wait_ge(*done("ln2_T_copy", b, TT - 1))
                            pe.wait_ge(shared_in[f % 2], 16 * (b * KF // 2 + f // 2 + 1))
                        ps = banks[BANK[(f"{task}_lo", f)]]
                        for k in (range(KD // 2) if lo else range(KD // 2, KD)):
                            last = MM(ps[:, :], shw[:, f % 2, which, k * P:(k + 1) * P], xT[:, k, :], start=(k == 0), stop=(k == KD - 1))
                        if not lo:
                            last.then_inc(S[task], 1)
                    return run

                def down(lo):
                    def run(b, t):
                        if lo:
                            bank("ffn_down_lo", b, t)
                            pe.wait_ge(*done("ffn_h", b, KF - 1))
                        pe.wait_ge(down_in[0 if lo else 1], 16 * (b + 1))
                        ps = banks[BANK[("ffn_down_lo", t)]]
                        for f in (range(KF // 2) if lo else range(KF // 2, KF)):
                            last = MM(ps[:, :], hT[:, f, t * P:(t + 1) * P], sh_down[:, f * D:(f + 1) * D], start=(f == 0), stop=(f == KF - 1))
                        if not lo:
                            last.then_inc(S["ffn_down"], 1)
                    return run

                tasks = dict(in_proj=in_proj, x_proj=x_proj, dt_proj=dt_proj, b_bcast=b_bcast, ln0_T=ln0_T, c_proj=c_proj,
                             c_T=c_T, qk=qk, qk_rolled=qk_rolled, v=v, score=score_, p_T=p_T, pv=pv, attn_out=attn_out, y_T=y_T,
                             ln2_T=ln2_T, logits=logits, earlier=earlier, ffn_gate_lo=ffn_in(0, "ffn_gate", True),
                             ffn_gate=ffn_in(0, "ffn_gate", False), ffn_up_lo=ffn_in(1, "ffn_up", True),
                             ffn_up=ffn_in(1, "ffn_up", False), ffn_down_lo=down(True), ffn_down=down(False))

                def c_bcast(k):
                    b, n = k // STEPS, k % NS
                    if k >= N_CB:
                        pe.wait_ge(S["times_c"], k - N_CB + 1)
                    if k % STEPS == 0:
                        pe.wait_ge(*done("split", b, N_SPLIT - 1))
                    MM(cb_ps[k % N_CB][:, :], pick[:, NS + n:NS + n + 1].to_broadcast([96, P]), bc_parts[:, b % 2, :],
                       start=True, stop=True).then_inc(S["c_bcast"], 1)

                def state_sum(k):
                    n, m = k % NS, k // NS
                    pe.wait_ge(S["times_c"], k + 1)
                    if n == 0 and m:
                        pe.wait_ge(S["y_sum"], m)
                    MM(y_ps[:, :], ident, state_c[:, k % N_HC, :], start=(n == 0), stop=(n == NS - 1)).then_inc(S["state_sum"], 1)

                for phase in range(-1, B + 2):
                    for step in range(STEPS):
                        if (phase, step) == FOLD_AT:
                            fold()
                        k = phase * STEPS + step
                        if k == 0:
                            c_bcast(0)
                        if 0 <= k < NK:
                            if k + 1 < NK:
                                c_bcast(k + 1)
                        if 0 <= k - 1 < NK:
                            state_sum(k - 1)
                        for task, b, i in side_work("pe", phase, step):
                            tasks[task](b, i)

        expert_block(nc, stack, expert_w, const_f, out, rows_dram)


N_W, N_X = 4, 2
F2 = 2 * FE
WCOLS = KD * F2 + FE // P * D


def expert_block(nc, stack, expert_w, const_f, out, rows_dram):
    def sem(name):
        return stack.enter_context(nc.semaphore(name))

    w_in = [sem(f"expert_w_in{i}") for i in range(N_W)]
    r_in = [sem(f"expert_rows_in{i}") for i in range(N_W)]
    iota_in, turned, turned_copy = sem("iota_in"), sem("rows_turned"), sem("rows_turned_copy")
    hidden, tanh_done, silu_done, h_done = sem("hidden"), sem("hidden_tanh"), sem("hidden_silu"), sem("h_done")
    h_turned, h_turned_copy, down = sem("h_turned"), sem("h_turned_copy"), sem("down")
    picked, w_done, ids, down_copy, added = sem("picked"), sem("row_weight"), sem("row_token"), sem("down_copy"), sem("added")

    def sb(name, shape, dt=F32):
        return stack.enter_context(nc.sbuf_tensor(name, shape, dt))

    wts = sb("ex_w", [P, N_W, WCOLS])
    rows = sb("ex_rows", [P, N_W, ROW])
    cid = sb("ex_cid", [P, P + E])
    ident, iota = cid[:, 0:P], cid[:, P:P + E]
    rowsT = sb("ex_rowsT", [P, N_X, D])
    th = sb("ex_th", [P, N_X, FE])
    sl = sb("ex_silu", [P, N_X, FE])
    h = sb("ex_h", [P, N_X, FE])
    hT = sb("ex_hT", [P, N_X, FE])
    ob = sb("ex_out", [P, N_X, D])
    w4 = sb("ex_w4", [P, N_X, TOPK])
    wt = sb("ex_weight", [P, N_X])
    tok = sb("ex_token", [P, N_W], U32)
    ps = [stack.enter_context(nc.psum_tensor(f"ex_bank{i}", [P, 512], F32)) for i in range(8)]
    turn_ps, hid_ps, ht_ps, down_ps = ps[0:2], ps[2:4], ps[4:6], ps[6:8]

    def all_experts(engine, body):
        for e in range(N_W):
            body(e, e, False, N_W)
        with engine.Fori(N_W, E - N_W, N_W) as e0:
            for j in range(N_W):
                body(e0 + j, j, True, N_W)
        for e in range(E - N_W, E):
            body(e, e % N_W, True, E - 1 - e)

    block = stack.enter_context(nc.Block())

    @block.sync
    def _(sp):
        sp.dma_start(cid[:, 0:P], const_f[:, 0:P]).then_inc(iota_in, 16)
        sp.dma_start(cid[:, P:P + E], const_f[:, 2 * P + 2 * T:2 * P + 2 * T + E]).then_inc(iota_in, 16)

        def load(e, j, again, left):
            if again:
                sp.wait_ge(down, e - N_W + 1)
                sp.wait_ge(ids, e - N_W + 1)
            sp.dma_start(rows[:, j, :], rows_dram[bass.ts(e, CAP), :]).then_inc(r_in[j], 16)
            sp.dma_start(wts[:, j, :], expert_w[bass.ts(e, P), :]).then_inc(w_in[j], 16)

        all_experts(sp, load)

    @block.tensor
    def _(pe):
        MM = nc.tensor.matmul

        def rows_in(e, j, again):
            pe.wait_ge(r_in[j], (e - j) * (16 // N_W) + 16)
            if again or j >= N_X:
                pe.wait_ge(turned_copy, e - N_X + 1)
            for k in range(KD):
                last = nc.tensor.transpose(turn_ps[j % N_X][:, k * P:(k + 1) * P], rows[:, j, k * P:(k + 1) * P], ident)
            last.then_inc(turned, 1)

        def gate_and_up(e, j, again, half):
            if half == 0:
                pe.wait_ge(w_in[j], (e - j) * (16 // N_W) + 16)
                pe.wait_ge(turned_copy, e + 1)
                if again or j >= N_X:
                    pe.wait_ge(h_done, e - N_X + 1)
            for k in range(half * KD // 2, (half + 1) * KD // 2):
                last = MM(hid_ps[j % N_X][:, :], rowsT[:, j % N_X, k * P:(k + 1) * P], wts[:, j, k * F2:(k + 1) * F2],
                          start=(k == 0), stop=(k == KD - 1))
            if half == 1:
                last.then_inc(hidden, 1)

        def run(e, j, again, left):
            def ahead(n):
                return e + n, (j + n) % N_W, again or j + n >= N_W
            if left >= 1:
                gate_and_up(*ahead(1), 0)
            pe.wait_ge(h_done, e + 1)
            if again or j >= N_X:
                pe.wait_ge(h_turned_copy, e - N_X + 1)
            for k in range(FE // P):
                last = nc.tensor.transpose(ht_ps[j % N_X][:, k * P:(k + 1) * P], h[:, j % N_X, k * P:(k + 1) * P], ident)
            last.then_inc(h_turned, 1)
            if left >= 1:
                gate_and_up(*ahead(1), 1)
            if left >= 2:
                rows_in(*ahead(2))
            pe.wait_ge(h_turned_copy, e + 1)
            if again or j >= N_X:
                pe.wait_ge(down_copy, e - N_X + 1)
            for k in range(FE // P):
                last = MM(down_ps[j % N_X][:, :], hT[:, j % N_X, k * P:(k + 1) * P],
                          wts[:, j, KD * F2 + k * D:KD * F2 + (k + 1) * D], start=(k == 0), stop=(k == FE // P - 1))
            last.then_inc(down, 1)

        pe.wait_ge(iota_in, 32)
        rows_in(0, 0, False)
        gate_and_up(0, 0, False, 0)
        gate_and_up(0, 0, False, 1)
        rows_in(1, 1, False)
        all_experts(pe, run)

    @block.scalar
    def _(act):
        def copy_rows(e, j, again):
            act.wait_ge(turned, e + 1)
            if again or j >= N_X:
                act.wait_ge(hidden, e - N_X + 1)
            nc.scalar.copy(rowsT[:, j % N_X, :], turn_ps[j % N_X][:, :]).then_inc(turned_copy, 1)

        def run(e, j, again, left):
            act.wait_ge(hidden, e + 1)
            if again or j >= N_X:
                act.wait_ge(silu_done, e - N_X + 1)
            nc.scalar.activation(th[:, j % N_X, :], hid_ps[j % N_X][:, 0:FE], ACT.Tanh, scale=0.5).then_inc(tanh_done, 1)
            if left:
                copy_rows(e + 1, (j + 1) % N_W, again or j + 1 == N_W)
            act.wait_ge(h_turned, e + 1)
            if again or j >= N_X:
                act.wait_ge(down, e - N_X + 1)
            nc.scalar.copy(hT[:, j % N_X, :], ht_ps[j % N_X][:, 0:FE]).then_inc(h_turned_copy, 1)

        copy_rows(0, 0, False)
        all_experts(act, run)

    @block.vector
    def _(dve):
        V = nc.vector
        dve.wait_ge(iota_in, 32)

        def run(e, j, again, left):
            i = j % N_X
            dve.wait_ge(r_in[j], (e - j) * (16 // N_W) + 16)
            if again or j >= N_X:
                dve.wait_ge(h_done, e - N_X + 1)
            V.scalar_tensor_tensor(w4[:, i, :], rows[:, j, E_AT:E_AT + TOPK], iota[:, bass.ds(e, 1)],
                                   rows[:, j, W_AT:W_AT + TOPK], ALU.is_equal, ALU.mult).then_inc(picked, 1)
            dve.wait_ge(picked, e + 1)
            V.tensor_reduce(wt[:, i:i + 1], w4[:, i, :], AX_X, ALU.add).then_inc(w_done, 1)
            if again:
                dve.wait_ge(added, 16 * (e - N_W + 1))
            V.tensor_copy(tok[:, j:j + 1], rows[:, j, ID_AT:ID_AT + 1]).then_inc(ids, 1)
            dve.wait_ge(tanh_done, e + 1)
            V.scalar_tensor_tensor(sl[:, i, :], th[:, i, :], 1.0, hid_ps[i][:, 0:FE], ALU.add, ALU.mult).then_inc(silu_done, 1)
            dve.wait_ge(silu_done, e + 1)
            if again or j >= N_X:
                dve.wait_ge(h_turned, e - N_X + 1)
            V.scalar_tensor_tensor(h[:, i, :], sl[:, i, :], wt[:, i:i + 1], hid_ps[i][:, FE:F2], ALU.mult, ALU.mult).then_inc(h_done, 1)
            if again or j >= 1:
                copy_out(e - 1, (j - 1) % N_X, again or j >= 1 + N_X)

        def copy_out(e, i, again):
            dve.wait_ge(down, e + 1)
            if again:
                dve.wait_ge(added, 16 * (e - N_X + 1))
            V.tensor_copy(ob[:, i, :], down_ps[i][:, :]).then_inc(down_copy, 1)

        all_experts(dve, run)
        copy_out(E - 1, (E - 1) % N_X, True)

    @block.gpsimd
    def _(pool):
        def run(e, j, again, left):
            pool.wait_ge(down_copy, e + 1)
            pool.wait_ge(ids, e + 1)
            if again or j >= 1:
                pool.wait_ge(added, 16 * e)
            nc.gpsimd.indirect_dma_start(
                out=out, out_offset=bass.IndirectOffsetOnAxis(ap=tok[:, j:j + 1], axis=0),
                in_=ob[:, j % N_X, :], in_offset=None, bounds_check=B * T + P - 1,
                compute_op=ALU.add).then_inc(added, 16)

        for e in range(E):
            run(e, e % N_W, e >= N_W, E - 1 - e)
        pool.wait_ge(added, 16 * E)


def kernel(**inputs):
    import ml_dtypes
    import concourse.bacc as bacc
    from concourse.bass_utils import run_bass_kernel_spmd

    a = {k: np.asarray(v) for k, v in inputs.items()}

    def rows(w, p=P):
        return w.reshape(-1, p, w.shape[-1]).transpose(1, 0, 2)

    def flat(parts):
        return np.concatenate([p.reshape(p.shape[0], -1) for p in parts], axis=1)

    wq, wkv = a["L0_attn_W_q_comp"], a["L0_attn_W_kv_comp"]
    wk, wv = wkv[:DC], wkv[DC:]
    lat_w = flat([a["L0_attn_W_to_kv"], a["L0_attn_W_out_res"].T])
    gamma_beta = np.zeros((P, 2), np.float32)
    gamma_beta[:DC, 0], gamma_beta[:DC, 1] = a["L0_attn_ln_gamma"], a["L0_attn_ln_beta"]
    comp_w = flat([a["L0_attn_W_compress"].T, a["L0_attn_W_comp2lat"], gamma_beta])
    roll = lambda w: np.roll(w, -DC // 2, axis=0)
    qk_w = flat([wq.T, wk.T, roll(wq).T, roll(wk).T, wv.T])
    xp = a["L0_xattn_x_proj_w"]
    xp_pad = np.zeros((DC, DI), np.float32)
    xp_pad[0:RK], xp_pad[2 * RK:] = xp[:RK], xp[RK:]
    chan = flat([a["L0_xattn_conv_w"][:, 0, :], a["L0_xattn_conv_b"][:, None], a["L0_xattn_dt_proj_b"][:, None],
                 a["L0_xattn_D"][:, None], a["L0_xattn_A_log"]])
    token_b = np.broadcast_to(np.concatenate([a["L0_attn_b_out_res"], a["L0_ffn_gate_bias"]])[None], (P, D + E))
    gate_up = np.stack([rows(a["L0_ffn_shared_gate"]), rows(a["L0_ffn_shared_up"])], axis=1)
    gate_up = gate_up.reshape(P, 2, KD, KF, P).transpose(0, 3, 1, 2, 4)
    shared_w = flat([gate_up, rows(a["L0_ffn_shared_down"])])
    w13 = np.concatenate([a["L0_ffn_w1"], a["L0_ffn_w3"]], axis=2)
    w13 = w13.reshape(E, KD, P, F2).transpose(0, 2, 1, 3).reshape(E * P, KD * F2)
    w2 = a["L0_ffn_w2"].reshape(E, FE // P, P, D).transpose(0, 2, 1, 3).reshape(E * P, FE // P * D)

    f32 = np.float32
    inv = (1.0 / f32(10000.0) ** (np.arange(0, DC, 2, dtype=f32) / f32(DC))).astype(f32)
    angle = (np.arange(T, dtype=f32)[:, None] * inv[None, :]).astype(f32).T
    cos = np.tile(np.cos(angle), (4, 1))
    sin = np.concatenate([-np.sin(angle), np.sin(angle)] * 2)
    mask = np.where(np.tril(np.ones((P, P), bool)), 0.0, NEG)
    line = np.arange(P)
    every = lambda v: np.broadcast_to(np.asarray(v)[None, :], (P, len(v)))
    spare = np.broadcast_to((B * T + line)[:, None], (P, E))
    token = line[:, None] + P * np.arange(B * TT)[None, :]
    const_f = flat([np.eye(P), mask, cos, sin, every(np.arange(E)), every(np.arange(E) // (E // G)), spare, token]).astype(f32)
    const_b = flat([np.triu(np.ones((P, P)), 1), np.ones((P, P)), line[:, None] % E == np.arange(E)[None]]).astype(ml_dtypes.bfloat16)

    arrays = {
        "x_in": a["x"].reshape(B, TT, P, D),
        "ctx_t": a["ctx_1024"].transpose(0, 2, 1).reshape(B, DCTX // P, P, T).transpose(0, 2, 1, 3),
        "lat_w": lat_w, "comp_w": comp_w, "qk_w": qk_w,
        "in_w": rows(a["L0_xattn_in_proj_w"].T), "xp_w": rows(xp_pad.T), "dtp_w": a["L0_xattn_dt_proj_w"].T,
        "chan": rows(chan), "gate_w": rows(a["L0_ffn_gate_w"].T), "token_b": token_b,
        "shared_w": shared_w, "expert_w": np.concatenate([w13, w2], axis=1),
        "const_f": const_f, "const_b": const_b,
    }
    arrays = {k: np.ascontiguousarray(v) for k, v in arrays.items()}
    nc = bacc.Bacc("TRN2", target_bir_lowering=False, num_devices=1)
    args = [nc.dram_tensor(k, v.shape, mybir.dt.from_np(v.dtype), kind="ExternalInput").ap() for k, v in arrays.items()]
    out = nc.dram_tensor("out", (B * T + P, D), F32, kind="ExternalOutput").ap()
    rows_dram = nc.dram_tensor("rows_dram", (E * CAP, ROW), F32, kind="Internal").ap()
    decoder_layer(nc, *args, out, rows_dram)
    r = run_bass_kernel_spmd(nc, [arrays], core_ids=[0])
    return r.results[0]["out"][:B * T].reshape(B, T, D)
```
